# Optimizing a Trainium2 kernel written in Bass

```python
import numpy as np
import jax
import jax.numpy as jnp

def _softmax(x, axis=-1):
    return jax.nn.softmax(x, axis=axis)

def _gelu(x):
    return jax.nn.gelu(x, approximate=True)

def _silu(x):
    return jax.nn.silu(x)

def _sigmoid(x):
    return jax.nn.sigmoid(x)

def _layernorm(x, axis=-1, eps=1e-05):
    m = jnp.mean(x, axis=axis, keepdims=True)
    v = jnp.var(x, axis=axis, keepdims=True)
    return (x - m) / jnp.sqrt(v + eps)

def _scatter_add(tgt, idx, src, axis=0):
    return tgt.at[idx].add(src)

def _segment_sum(src, seg, n):
    return jax.ops.segment_sum(src, seg, n)
kernel_name = 'mk_adaln_d1_jaxref_r8_2fb08e'

def setup_inputs(seed: int=0):
    np.random.seed(seed)
    _w = jnp.asarray

    def _L0_attn_setup():
        import jax, jax.numpy as jnp
        import numpy as np
        B, T = (2, 256)
        DENSE = 128
        SPARSE = 128
        NH = 8
        HD = SPARSE // NH
        WINDOW = 64
        K = 32
        RANK = HD // 4
        GATE_THRESH = 0.2

        def _causal_window_indices(t_len, window):
            pos = jnp.arange(t_len)
            off = jnp.arange(window)
            idx = jnp.clip(pos[:, None] - off[None, :], 0, t_len - 1)
            mask = idx <= pos[:, None]
            return (idx, mask)

        def _dynamic_metric(field, w1, b1, w2, b2, base):
            sig = field.mean(axis=1)
            if field.shape[1] >= 8:
                sig = sig + field[:, ::8].mean(axis=1) * 0.5
            h = jax.nn.gelu(sig @ w1 + b1, approximate=False)
            mod = (h @ w2 + b2).reshape(field.shape[0], NH, HD)
            return jax.nn.softplus(base[None] + 0.1 * mod)
        key = jax.random.key(seed)
        ks = jax.random.split(key, 12)
        return {'x': jax.random.normal(ks[0], (B, T, DENSE), dtype=jnp.float32), 'enc_q': jax.random.normal(ks[1], (NH, DENSE, HD), dtype=jnp.float32) * 0.02, 'enc_v': jax.random.normal(ks[2], (NH, DENSE, HD), dtype=jnp.float32) * 0.02, 'metric_w1': jax.random.normal(ks[3], (SPARSE, SPARSE // 2), dtype=jnp.float32) * (1.0 / np.sqrt(SPARSE)), 'metric_b1': jnp.zeros((SPARSE // 2,), dtype=jnp.float32), 'metric_w2': jax.random.normal(ks[4], (SPARSE // 2, NH * HD), dtype=jnp.float32) * (1.0 / np.sqrt(SPARSE // 2)), 'metric_b2': jnp.zeros((NH * HD,), dtype=jnp.float32), 'base_metric': jnp.ones((NH, HD), dtype=jnp.float32) * 0.1, 'hebb_U': jax.random.normal(ks[5], (NH, HD, RANK), dtype=jnp.float32) * 0.01, 'hebb_V': jax.random.normal(ks[6], (NH, RANK, HD), dtype=jnp.float32) * 0.01, 'decoder': jax.random.normal(ks[7], (NH * HD, DENSE), dtype=jnp.float32) * 0.02}
    _L0_attn_in = _L0_attn_setup()

    def _L0_ffn_setup():
        import jax, jax.numpy as jnp
        import numpy as np
        B, L, H = (8, 256, 128)
        E, K, R = (8, 2, 64)

        def _gates(cls_tok, Wr):
            logits = cls_tok @ Wr.T
            top_vals, top_idx = jax.lax.top_k(logits, K)
            neg_inf = jnp.full_like(logits, -jnp.inf)
            rows = jnp.arange(logits.shape[0])[:, None]
            masked = neg_inf.at[rows, top_idx].set(top_vals)
            return jax.nn.softmax(masked, axis=-1)
        key = jax.random.key(seed)
        k1, k2, k3, k4 = jax.random.split(key, 4)
        x = jax.random.normal(k1, (B, L, H), dtype=jnp.float32)
        Wr = jax.random.normal(k2, (E, H), dtype=jnp.float32) * (1.0 / np.sqrt(H))
        A = jax.random.normal(k3, (E, R, H), dtype=jnp.float32) * (1.0 / np.sqrt(H))
        Bw = jax.random.normal(k4, (E, H, R), dtype=jnp.float32) * (1.0 / np.sqrt(R))
        return {'x': x, 'Wr': Wr, 'A': A, 'Bw': Bw}
    _L0_ffn_in = _L0_ffn_setup()
    _L0_c = _w((lambda *s: np.random.randn(*s).astype(np.float32) * 0.05)(8, 128))
    _L0_wmod = _w((lambda *s: np.random.randn(*s).astype(np.float32) * 0.05)(128, 6 * 128) * 128 ** (-0.5))
    _d = {'L0_attn_x': _L0_attn_in['x'], 'L0_attn_enc_q': _L0_attn_in['enc_q'], 'L0_attn_enc_v': _L0_attn_in['enc_v'], 'L0_attn_metric_w1': _L0_attn_in['metric_w1'], 'L0_attn_metric_b1': _L0_attn_in['metric_b1'], 'L0_attn_metric_w2': _L0_attn_in['metric_w2'], 'L0_attn_metric_b2': _L0_attn_in['metric_b2'], 'L0_attn_base_metric': _L0_attn_in['base_metric'], 'L0_attn_hebb_U': _L0_attn_in['hebb_U'], 'L0_attn_hebb_V': _L0_attn_in['hebb_V'], 'L0_attn_decoder': _L0_attn_in['decoder'], 'L0_ffn_Wr': _L0_ffn_in['Wr'], 'L0_ffn_A': _L0_ffn_in['A'], 'L0_ffn_Bw': _L0_ffn_in['Bw'], 'L0_c': _L0_c, 'L0_wmod': _L0_wmod}
    _x0 = _d['L0_attn_x']
    _d['L0_attn_x'] = jax.random.normal(jax.random.fold_in(jax.random.key(seed), 1), (8, 1024, 128), dtype=_x0.dtype)
    del _x0
    return _d

def reference(L0_attn_x, L0_attn_enc_q, L0_attn_enc_v, L0_attn_metric_w1, L0_attn_metric_b1, L0_attn_metric_w2, L0_attn_metric_b2, L0_attn_base_metric, L0_attn_hebb_U, L0_attn_hebb_V, L0_attn_decoder, L0_ffn_Wr, L0_ffn_A, L0_ffn_Bw, L0_c, L0_wmod):

    def _L0_attn_ref(x, enc_q, enc_v, metric_w1, metric_b1, metric_w2, metric_b2, base_metric, hebb_U, hebb_V, decoder):
        import jax, jax.numpy as jnp
        import numpy as np
        B, T = (2, 256)
        DENSE = 128
        SPARSE = 128
        NH = 8
        HD = SPARSE // NH
        WINDOW = 64
        K = 32
        RANK = HD // 4
        GATE_THRESH = 0.2

        def _causal_window_indices(t_len, window):
            pos = jnp.arange(t_len)
            off = jnp.arange(window)
            idx = jnp.clip(pos[:, None] - off[None, :], 0, t_len - 1)
            mask = idx <= pos[:, None]
            return (idx, mask)

        def _dynamic_metric(field, w1, b1, w2, b2, base):
            sig = field.mean(axis=1)
            if field.shape[1] >= 8:
                sig = sig + field[:, ::8].mean(axis=1) * 0.5
            h = jax.nn.gelu(sig @ w1 + b1, approximate=False)
            mod = (h @ w2 + b2).reshape(field.shape[0], NH, HD)
            return jax.nn.softplus(base[None] + 0.1 * mod)
        Bb, Tt, _ = x.shape
        query_sparse = jax.nn.relu(jnp.einsum('btd,nde->btne', x, enc_q))
        value_sparse = jax.nn.relu(jnp.einsum('btd,nde->btne', x, enc_v))
        metric = _dynamic_metric(query_sparse.reshape(Bb, Tt, NH * HD), metric_w1, metric_b1, metric_w2, metric_b2, base_metric)
        idx, mask = _causal_window_indices(Tt, WINDOW)
        idx_b = jnp.broadcast_to(idx[None], (Bb, Tt, WINDOW))
        batch_ix = jnp.arange(Bb)[:, None, None]
        outs = []
        for h in range(NH):
            q_h = query_sparse[:, :, h, :]
            v_h = value_sparse[:, :, h, :]
            m_h = metric[:, h][:, None, None, :]
            k_windows = q_h[:, idx, :]
            diff = k_windows - q_h[:, :, None, :]
            dist = jnp.sqrt((diff * diff * m_h).sum(axis=-1) + 1e-08)
            dist = jnp.where(mask[None], dist, jnp.inf)
            neg_d, loc = jax.lax.top_k(-dist, K)
            topd = -neg_d
            top_idx = jnp.take_along_axis(idx_b, loc, axis=2)
            infl = jnp.exp(-topd)
            infl = infl / (infl.sum(axis=-1, keepdims=True) + 1e-08)
            neighbor_v = v_h[batch_ix, top_idx]
            context = jnp.einsum('btk,btkd->btd', infl, neighbor_v)
            q_norm = jnp.linalg.norm(q_h, axis=-1, keepdims=True)
            gate = (q_norm > GATE_THRESH).astype(q_h.dtype)
            heb_mat = hebb_U[h] @ hebb_V[h]
            q_unit = q_h / jnp.maximum(q_norm, 1e-12)
            heb_ctx = q_unit @ heb_mat
            context = context + gate * 0.1 * heb_ctx
            outs.append(q_h * context)
        out_sparse = jnp.stack(outs, axis=2)
        return out_sparse.reshape(Bb, Tt, NH * HD) @ decoder

    def _L0_ffn_ref(x, Wr, A, Bw):
        import jax, jax.numpy as jnp
        import numpy as np
        B, L, H = (8, 256, 128)
        E, K, R = (8, 2, 64)

        def _gates(cls_tok, Wr):
            logits = cls_tok @ Wr.T
            top_vals, top_idx = jax.lax.top_k(logits, K)
            neg_inf = jnp.full_like(logits, -jnp.inf)
            rows = jnp.arange(logits.shape[0])[:, None]
            masked = neg_inf.at[rows, top_idx].set(top_vals)
            return jax.nn.softmax(masked, axis=-1)
        gates = _gates(x[:, 0, :], Wr)
        mid = jnp.einsum('blh,erh->belr', x, A)
        expert_out = jnp.einsum('belr,ehr->belh', mid, Bw)
        weighted = jnp.einsum('be,belh->blh', gates, expert_out)
        return x + weighted
    x = L0_attn_x
    mod = (_silu(L0_c) @ L0_wmod).reshape(L0_c.shape[0], 6, 1, -1)
    sa, ca, ga, sb, cb, gb = (mod[:, 0], mod[:, 1], mod[:, 2], mod[:, 3], mod[:, 4], mod[:, 5])
    ga = (2 * (ga >= 0) - 1) * jnp.maximum(jnp.abs(ga), 0.25)
    gb = (2 * (gb >= 0) - 1) * jnp.maximum(jnp.abs(gb), 0.25)
    h = _layernorm(x, axis=-1) * (1 + ca) + sa
    x = x + ga * _L0_attn_ref(h, L0_attn_enc_q, L0_attn_enc_v, L0_attn_metric_w1, L0_attn_metric_b1, L0_attn_metric_w2, L0_attn_metric_b2, L0_attn_base_metric, L0_attn_hebb_U, L0_attn_hebb_V, L0_attn_decoder)
    h = _layernorm(x, axis=-1) * (1 + cb) + sb
    x = x + gb * _L0_ffn_ref(h, L0_ffn_Wr, L0_ffn_A, L0_ffn_Bw)
    return x

_drawn_inputs = setup_inputs


def setup_inputs(seed=0):
    import zlib

    import numpy as np

    out = dict(_drawn_inputs(seed))
    spreads = {'L0_attn_metric_b1': (0.0, 2.0),
     'L0_attn_metric_b2': (0.0, 2.0),
     'L0_attn_base_metric': (0.10000000149011612, 0.6)}
    factors = {'L0_attn_enc_q': 8.0,
     'L0_attn_enc_v': 8.0,
     'L0_attn_metric_w1': 8.0,
     'L0_attn_metric_w2': 8.0,
     'L0_attn_hebb_U': 64.0,
     'L0_attn_hebb_V': 64.0,
     'L0_attn_decoder': 8.0}
    for name, (base, spread) in spreads.items():
        noise = np.random.default_rng([zlib.crc32(name.encode()), seed]).standard_normal(out[name].shape)
        drawn = base * np.exp(spread * noise) if base else spread * noise
        out[name] = jnp.asarray(drawn.astype(out[name].dtype))
    for name, factor in factors.items():
        out[name] = (out[name] * factor).astype(out[name].dtype)
    return out
```

```python
from contextlib import ExitStack

import numpy as np

import concourse.bass as bass
from concourse import mybir

ALU = mybir.AluOpType
ACT = mybir.ActivationFunctionType
F32 = mybir.dt.float32
BF16 = mybir.dt.bfloat16
AX_X = mybir.AxisListType.X

P = 128
NB, T, D = 8, 1024, 128
NH, HD = 8, 16
WIN, TOPK = 64, 32
RANK = 4
NE, ER = 8, 64
NR, NG = 4, 2
TP = T + WIN
CH = P
NCH = NB * T // CH
CPB = T // CH
HALF = 512
VD = HD + 1
BIG = 1e30
EPS_LN = 1e-5
GATE2 = 0.2 * 0.2

C_ID = 0
C_MASK = C_ID + P
C_UNF = C_MASK + 4 * WIN
C_ROW = C_UNF + 2 * WIN
C_SELN = C_ROW + 3
C_SELQ = C_SELN + NG * NH
C_BLK = C_SELQ + NR * HD
C_EXP = C_BLK + NG * NR
C_END = C_EXP + NE * ER


def constants():
    c = np.zeros((P, C_END), np.float32)
    c[:, C_ID:C_ID + P] = np.eye(P, dtype=np.float32)
    i = (np.arange(P) % WIN)[:, None]
    late = (np.arange(P) >= WIN)[:, None]
    j = np.arange(WIN)[None, :]
    own = np.where(j > i, BIG, np.where(j == i, -BIG, 0.0))
    before = np.where(j > i, 0.0, BIG)
    a = np.where(late, before, own)
    b = np.where(late, own, before)
    c[:, C_MASK:C_MASK + 4 * WIN] = np.concatenate([a, a, b, b], 1)
    c[:, C_UNF:C_UNF + 2 * WIN] = np.concatenate([a, b], 1) <= 0
    e = np.arange(P) % 32
    r = np.arange(P) // 32
    c[:, C_ROW] = np.where(e < HD, -2.0, 0.0)
    c[:, C_ROW + 1] = e == HD + 1
    c[:, C_ROW + 2] = (e == HD) | (e == HD + 1)
    for p in range(P):
        if e[p] < HD:
            for g in range(NG):
                c[p, C_SELN + g * NH + NG * r[p] + g] = -0.5
            c[p, C_SELQ + r[p] * HD + e[p]] = 1.0
    for h in range(NH):
        c[h * RANK:(h + 1) * RANK, C_BLK + (h % NG) * NR + h // NG] = 1.0
    for x in range(NE):
        c[x, C_EXP + x * ER:C_EXP + (x + 1) * ER] = 1.0
    return c


def adaln_block(nc, x, encq, encv, w1, b1, w2, b2, base, hebu, hebv, dec, wr, amat, bmat, cin, wmod, consts, out):
    ctx = ExitStack()

    def sb(name, shape, dt=F32):
        return ctx.enter_context(nc.sbuf_tensor(name, shape, dt))

    def sem(name):
        return ctx.enter_context(nc.semaphore(name))

    with ctx:
        con = sb("con", [P, C_END])
        encq_sb = sb("encq_sb", [P, NG, P])
        encv_sb = sb("encv_sb", [P, P])
        w1_sb = sb("w1_sb", [P, NG, 64])
        b1_sb = sb("b1_sb", [64, 1])
        w2_sb = sb("w2_sb", [64, NG, P])
        b2_sb = sb("b2_sb", [P, NG])
        base_sb = sb("base_sb", [P, NG])
        hebu_sb = sb("hebu_sb", [NH * RANK, HD])
        hebv_sb = sb("hebv_sb", [NH * RANK, HD])
        dec_sb = sb("dec_sb", [P, D])
        wr_sb = sb("wr_sb", [P, NE])
        a_sb = sb("a_sb", [P, 4, D])
        b_sb = sb("b_sb", [P, 4, D])
        c_sb = sb("c_sb", [P, NB])
        wmod_sb = sb("wmod_sb", [P, 6 * D])
        x0_sb = sb("x0_sb", [NB, D])
        ident = con[:, C_ID:C_ID + P]
        seln = con[:, C_SELN:C_SELN + NG * NH].rearrange("p (g h) -> p g h", g=NG)
        unf = con[:, C_UNF:C_UNF + 2 * WIN].rearrange("p (v j) -> p v j", v=2)
        ident_bf = sb("ident_bf", [P, P], BF16)
        mask_bf = sb("mask_bf", [P, 4 * WIN], BF16)
        bias = sb("bias", [P, 4])
        hT_all = sb("hT_all", [P, NB * TP])
        qT_all = sb("qT_all", [P, NG, NB * TP])
        dec_b = sb("dec_b", [P, NB, D])
        g_b = sb("g_b", [P, NB, D])
        selheb = sb("selheb", [P, NG, 2, NR * HD])
        aS = sb("aS", [P, NG, NB])
        modT = sb("modT", [P, 6, NB])
        ec = sb("ec", [P, NB])
        sil = sb("sil", [P, NB])
        modn = sb("modn", [NB, 6 * D])
        gn = sb("gn", [NB, 2, D])
        gsgn = sb("gsgn", [NB, 2, D])
        gabs = sb("gabs", [NB, 2, D])
        gaw = sb("gaw", [P, 2, 2, D])
        udiag = sb("udiag", [NH * RANK, NG, NR, 32])
        vdiag = sb("vdiag", [NH * RANK, NG, NR, HD])
        ebuf = sb("ebuf", [P, 4, NH * WIN])
        xp = ebuf[:, 0:2].rearrange("p h (c d) -> p h c d", c=4)
        xn = ebuf[:, 2:4].rearrange("p h (c d) -> p h c d", c=4)
        st_p = sb("st_p", [P, 2, 4, 6])
        mv_p = sb("mv_p", [P, 2, 4, 2])
        rs_p = sb("rs_p", [P, 2, 4])
        qsum = sb("qsum", [P, NG, 2, NB])
        qsum8 = sb("qsum8", [P, NG, NB])
        sig = sb("sig", [P, NG, NB])
        h1 = sb("h1", [64, NB])
        sp = sb("sp", [P, 8, NG * NB])
        z8 = ebuf[0:NB].rearrange("p h (c d) -> p (h c) d", c=4)
        s8 = sb("s8", [NB, 24, 8])
        o0T = sb("o0T", [P, NB])
        h0T = sb("h0T", [P, NB])
        gateT = sb("gateT", [NE, NB])
        gate_er = sb("gate_er", [P, 4, NB])
        big = sb("big", [P, 2, 2, NH * CH])
        bsc = big[:].rearrange("p a s (b d) -> p (a s) b d", b=NB)
        hst = sb("hst", [P, 2, 3 * WIN])
        tst = sb("tst", [P, 2, NG, CH])
        sst = sb("sst", [P, 2, NG, 3 * WIN])
        sqs = sb("sqs", [P, 2, NG, 3 * WIN])
        nst = sb("nst", [NH, 2, 3 * WIN])
        work = sb("work", [P, 2, NH * WIN])
        m8 = sb("m8", [P, NH, 8])
        wsel = sb("wsel", [P, NH * WIN])
        wun = big[:, 0].rearrange("p s (h j) -> p s h j", h=NH)
        wts = big[:, 1].rearrange("p s (h t) -> p s h t", h=NH)
        vst = sb("vst", [P, 4, NH, 2, VD])
        qh = sb("qh", [P, 4, 2, P])
        cst = sb("cst", [P, 2, NH, VD])
        den = sb("den", [P, 2, NH])
        rden = sb("rden", [P, 2, NH])
        qsq = sb("qsq", [P, NH * HD])
        n2 = sb("n2", [P, 2, NH])
        n2g = sb("n2g", [P, 2, NH])
        lnn = sb("lnn", [P, NH])
        rnn = sb("rnn", [P, 2, NH])
        gat = sb("gat", [P, 2, NH])
        hsc = sb("hsc", [P, NH])
        t1 = sb("t1", [P, NH * HD])
        t2 = sb("t2", [P, NH * HD])
        osp = sb("osp", [P, 2, NH * HD])
        oT = sb("oT", [P, 2, CH])
        xs = sb("xs", [P, 4, D])
        x2 = sb("x2", [P, 2, D])
        st_c = sb("st_c", [P, 6])
        mv_c = sb("mv_c", [P, 2, 2])
        lv_c = sb("lv_c", [P, 1])
        rs_c = sb("rs_c", [P, 2])
        n_c = sb("n_c", [P, 2, D])
        h2T = sb("h2T", [P, 2, CH])
        yo = sb("yo", [P, 2, D])

        psD = ctx.enter_context(nc.psum_tensor("psD", [P, 4, 512], F32))
        psW = ctx.enter_context(nc.psum_tensor("psW", [P, 2, 512], F32))
        psC = ctx.enter_context(nc.psum_tensor("psC", [P, 512], F32))
        psX = ctx.enter_context(nc.psum_tensor("psX", [P, 512], F32))
        dA = psD[:, :, 0:2 * WIN]
        dB = psD[:, :, 2 * WIN:4 * WIN]
        pV = psD[:, 0, 256:512]
        pQH = psD[:, 1, 256:512]
        pC = psC[:, 0:NH * 2 * VD]
        pO = psC[:, 384:512]
        pAtt = psC[:, 256:384]
        pN2 = psX[:, 0:P]
        pY = psX[:, P:2 * P]
        pN = psW[0:NH, 0, 0:3 * WIN]

        con_in = sem("con_in")
        c_in = sem("c_in")
        wq_in = sem("wq_in")
        wts_in = sem("wts_in")
        bias_set = sem("bias_set")
        bf_set = sem("bf_set")
        ec_ready = sem("ec_ready")
        sil_ready = sem("sil_ready")
        pmod_ready = sem("pmod_ready")
        modT_ready = sem("modT_ready")
        modn_ready = sem("modn_ready")
        dve_chain = sem("dve_chain")
        pool_chain = sem("pool_chain")
        gates_n_ready = sem("gates_n_ready")
        pgate_ready = sem("pgate_ready")
        gaw_ready = sem("gaw_ready")
        decb_ready = sem("decb_ready")
        diag_ready = sem("diag_ready")
        pheb_ready = sem("pheb_ready")
        selheb_ready = sem("selheb_ready")
        xp_in = [sem("xp_in0"), sem("xp_in1")]
        mv_ready = sem("mv_ready")
        lnv_p = sem("lnv_p")
        rs_ready = sem("rs_ready")
        st_ready = sem("st_ready")
        xn_ready = sem("xn_ready")
        pT_ready = sem("pT_ready")
        hT_ready = sem("hT_ready")
        pq_ready = sem("pq_ready")
        q_ready = sem("q_ready")
        qsum8_ready = sem("qsum8_ready")
        pads_ready = sem("pads_ready")
        sig_ready = sem("sig_ready")
        pm1_ready = sem("pm1_ready")
        h1_ready = sem("h1_ready")
        pm2_ready = sem("pm2_ready")
        z_ready = sem("z_ready")
        sp_act = sem("sp_act")
        sp_dve = sem("sp_dve")
        aS_ready = sem("aS_ready")
        p0_ready = sem("p0_ready")
        r0_act = sem("r0_act")
        r0_dve = sem("r0_dve")
        r0_pe = sem("r0_pe")
        gb_free = sem("gb_free")
        bsc_ready = sem("bsc_ready")
        pG_ready = sem("pG_ready")
        gb_ready = sem("gb_ready")
        ones_set = sem("ones_set")
        waits_alone = sem("waits_alone")
        opnd_ready = sem("opnd_ready")
        s_ready = sem("s_ready")
        pn_ready = sem("pn_ready")
        nst_ready = sem("nst_ready")
        rows_in = sem("rows_in")
        dist_ready = sem("dist_ready")
        amin_ready = sem("amin_ready")
        d2_ready = sem("d2_ready")
        ln_done = sem("ln_done")
        e_ready = sem("e_ready")
        vst_ready = sem("vst_ready")
        qhs_ready = sem("qhs_ready")
        picked = sem("picked")
        wsel_done = sem("wsel_done")
        w_ready = sem("w_ready")
        wt_ready = sem("wt_ready")
        wts_ready = sem("wts_ready")
        c_ready = sem("c_ready")
        cst_ready = sem("cst_ready")
        den_done = sem("den_done")
        rden_ready = sem("rden_ready")
        qsq_ready = sem("qsq_ready")
        n2_ready = sem("n2_ready")
        n2g_ready = sem("n2g_ready")
        lnn_done = sem("lnn_done")
        rnn_ready = sem("rnn_ready")
        mix_step = sem("mix_step")
        osp_ready = sem("osp_ready")
        po_ready = sem("po_ready")
        oT_ready = sem("oT_ready")
        att_ready = sem("att_ready")
        xs_in = [sem(f"xs_in{i}") for i in range(4)]
        x2_ready = sem("x2_ready")
        stc_ready = sem("stc_ready")
        mvc_ready = sem("mvc_ready")
        lnc_done = sem("lnc_done")
        rsc_ready = sem("rsc_ready")
        nc_ready = sem("nc_ready")
        pn2_ready = sem("pn2_ready")
        h2T_ready = sem("h2T_ready")
        y_ready = sem("y_ready")
        yo_ready = sem("yo_ready")
        out_in = [sem("out_in0"), sem("out_in1")]

        def need(eng, s, value):
            if isinstance(value, int) and value <= 0:
                return
            eng.wait_ge(s, value)

        def wait_alone(eng, s, value):
            if isinstance(value, int) and value <= 0:
                return
            eng.wait_ge(s, value)
            if not isinstance(value, int):
                eng.sem_inc(waits_alone, 1)

        FIRST, LAST = -3, NCH + 1
        LOOP0, LOOP1, UNROLL = 4, 57, 4

        def steps(eng, step):
            for i in range(FIRST, LOOP0):
                step(i, i % UNROLL)
            with eng.Fori(LOOP0, LOOP1, UNROLL) as i0:
                for u in range(UNROLL):
                    step(i0 + u, (LOOP0 + u) % UNROLL)
            for i in range(LOOP1 + UNROLL - 1, LAST + 1):
                step(i, i % UNROLL)

        def there(i, off):
            return not isinstance(i, int) or 0 <= i + off < NCH

        def column(k):
            return k * CH + (k // CPB) * WIN

        block = ctx.enter_context(nc.Block())

        @block.sync
        def _(sync):
            sync.dma_start(c_sb[:], cin).then_inc(c_in, 16)
            sync.dma_start(wmod_sb[:], wmod).then_inc(c_in, 16)
            sync.dma_start(con[:], consts).then_inc(con_in, 16)
            sync.dma_start(encq_sb[:], encq).then_inc(wq_in, 16)
            for dst, src in ((encv_sb, encv), (w1_sb, w1), (b1_sb, b1), (w2_sb, w2), (b2_sb, b2), (base_sb, base),
                             (hebu_sb, hebu), (hebv_sb, hebv), (dec_sb, dec), (wr_sb, wr), (a_sb, amat), (b_sb, bmat)):
                sync.dma_start(dst[:], src).then_inc(wts_in, 16)
            sync.dma_start(x0_sb[:], x.rearrange("(b t) d -> b t d", b=NB)[:, 0, :]).then_inc(wts_in, 16)
            xh = x.rearrange("(n c p) d -> p n c d", c=4, p=P)
            for half in range(2):
                sync.dma_start(xp[:, half], xh[:, half]).then_inc(xp_in[half], 16)
            with sync.Fori(1, NB) as b:
                for half in range(2):
                    sync.wait_ge(xn_ready, 2 * b - 1 + half)
                    sync.dma_start(xp[:, half], xh[:, bass.ds(2 * b + half, 1)].squeeze(1)).then_inc(xp_in[half], 16)

            xc = x.rearrange("(n p) d -> p n d", p=P)
            oc = out.rearrange("(n p) d -> p n d", p=P)

            def step(i, ph):
                k, s = i + 3, (ph + 3) % 2
                if there(i, 3):
                    sync.wait_ge(nst_ready, k + 1)
                    for g in range(NG):
                        n_g = nst[g:NH:NG, s]
                        sync.dma_start(sst[HD:P:32, s, g, :], n_g).then_inc(rows_in, 16)
                        sync.dma_start(tst[HD + 1:P:32, s, g, :], nst[g:NH:NG, s, WIN:3 * WIN]).then_inc(rows_in, 16)
                k = i + 1
                if there(i, 1):
                    need(sync, yo_ready, k - 3)
                    sync.dma_start(xs[:, (ph + 1) % 4], xc[:, bass.ds(k, 1)].squeeze(1)).then_inc(xs_in[(ph + 1) % 4], 16)
                k = i - 2
                if there(i, -2):
                    sync.wait_ge(yo_ready, k + 1)
                    sync.dma_start(oc[:, bass.ds(k, 1)].squeeze(1), yo[:, ph % 2]).then_inc(out_in[ph % 2], 16)

            steps(sync, step)
            for s in range(2):
                sync.wait_ge(out_in[s], 16 * NCH // 2)

        @block.gpsimd
        def _(pool):
            n = [0]

            def link(ins):
                n[0] += 1
                ins.then_inc(pool_chain, 1)
                pool.wait_ge(pool_chain, n[0])

            for col, value in enumerate((EPS_LN, 1e-8, 1.0, 0.0)):
                nc.gpsimd.memset(bias[:, col:col + 1], value).then_inc(bias_set, 1)
            nc.gpsimd.memset(udiag[:], 0.0).then_inc(ones_set, 1)
            for s in range(4):
                nc.gpsimd.memset(vst[:, s, :, :, HD:VD], 1.0).then_inc(ones_set, 1)
            pool.wait_ge(con_in, 16)
            nc.gpsimd.tensor_copy(ident_bf[:], ident).then_inc(bf_set, 1)
            nc.gpsimd.tensor_copy(mask_bf[:], con[:, C_MASK:C_MASK + 4 * WIN]).then_inc(bf_set, 1)
            pool.wait_ge(wts_in, 16 * 13)
            pool.wait_ge(ones_set, 1)
            hk = NH * RANK
            for g in range(NG):
                blk = con[0:hk, C_BLK + g * NR:C_BLK + (g + 1) * NR].unsqueeze(2).broadcast_to([hk, NR, HD])
                for dst, src in ((udiag[:, g, :, 0:HD], hebu_sb), (vdiag[:, g], hebv_sb)):
                    nc.gpsimd.tensor_tensor(dst, src[:].unsqueeze(1).broadcast_to([hk, NR, HD]), blk,
                                            ALU.mult).then_inc(diag_ready, 1)
            with pool.Fori(0, NB) as b:
                c0 = b * TP
                pool.wait_ge(hT_ready, 2 * b + 1)
                nc.gpsimd.tensor_copy(hT_all[:, bass.ds(c0, WIN)],
                                      hT_all[:, bass.ds(c0 + WIN, 1)].broadcast_to([P, WIN])).then_inc(pads_ready, 1)
                pool.wait_ge(q_ready, 4 * b + 2)
                nc.gpsimd.tensor_copy(qT_all[:, :, bass.ds(c0, WIN)],
                                      qT_all[:, :, bass.ds(c0 + WIN, 1)].broadcast_to([P, NG, WIN])).then_inc(pads_ready, 1)

            pool.wait_ge(aS_ready, 1)
            pool.wait_ge(pads_ready, 2 * NB)
            pool.wait_ge(q_ready, 4 * NB)

            def step(i, ph):
                k, s, s4 = i - 1, (ph - 1) % 2, (ph - 1) % 4
                if there(i, -1):
                    pool.wait_ge(picked, 16 * (k + 1))
                    need(pool, w_ready, k)
                    nc.gpsimd.tensor_tensor(wsel[:], ebuf[:, s4], work[:, s], ALU.subtract).then_inc(wsel_done, 1)
                    pool.wait_ge(wsel_done, k + 1)
                    need(pool, wt_ready, 8 * (k - 1))
                    nc.gpsimd.tensor_tensor(
                        wun[:, s].rearrange("p h (v j) -> p h v j", v=2),
                        wsel[:].rearrange("p (h j) -> p h j", h=NH).unsqueeze(2).broadcast_to([P, NH, 2, WIN]),
                        unf.unsqueeze(1).broadcast_to([P, NH, 2, WIN]), ALU.mult).then_inc(w_ready, 1)
                    pool.wait_ge(qhs_ready, k + 1)
                    need(pool, n2_ready, k)
                    nc.gpsimd.tensor_tensor(qsq[:], qh[:, s4, 0], qh[:, s4, 0], ALU.mult).then_inc(qsq_ready, 1)
                    pool.wait_ge(n2_ready, k + 1)
                    wait_alone(pool, mix_step, 4 * (k - 1))
                    nc.gpsimd.tensor_scalar(gat[:, s], n2[:, s], GATE2, 0.1, ALU.is_gt, ALU.mult).then_inc(n2g_ready, 1)
                    wait_alone(pool, rnn_ready, k - 1)
                    nc.gpsimd.tensor_scalar(n2g[:, s], n2[:, s], 1e-18, None, ALU.max).then_inc(n2g_ready, 1)
                    pool.wait_ge(rnn_ready, k + 1)
                    pool.wait_ge(n2g_ready, 2 * (k + 1))
                    nc.gpsimd.tensor_tensor(hsc[:], gat[:, s], rnn[:, s], ALU.mult).then_inc(mix_step, 1)
                    pool.wait_ge(rden_ready, k + 1)
                    pool.wait_ge(cst_ready, 2 * (k + 1))
                    h3 = "p (h e) -> p h e"
                    nc.gpsimd.tensor_tensor(t1[:].rearrange(h3, h=NH), cst[:, s, :, 0:HD],
                                            rden[:, s].unsqueeze(2).broadcast_to([P, NH, HD]), ALU.mult).then_inc(mix_step, 1)
                    pool.wait_ge(mix_step, 4 * k + 1)
                    nc.gpsimd.tensor_tensor(t2[:].rearrange(h3, h=NH), qh[:, s4, 1].rearrange(h3, h=NH),
                                            hsc[:].unsqueeze(2).broadcast_to([P, NH, HD]), ALU.mult).then_inc(mix_step, 1)
                    pool.wait_ge(mix_step, 4 * k + 3)
                    nc.gpsimd.tensor_tensor(t1[:], t1[:], t2[:], ALU.add).then_inc(mix_step, 1)
                    pool.wait_ge(mix_step, 4 * k + 4)
                    need(pool, po_ready, k - 1)
                    nc.gpsimd.tensor_tensor(osp[:, s], t1[:], qh[:, s4, 0], ALU.mult).then_inc(osp_ready, 1)
                k, s = i + 3, (ph + 3) % 2
                if there(i, 3):
                    b, c0 = k // CPB, column(k)
                    wait_alone(pool, dist_ready, k - 1)
                    win = qT_all[:, :, bass.ds(c0, 3 * WIN)]
                    nc.gpsimd.tensor_tensor(sst[:, s], win, aS[:, :, bass.ds(b, 1)].broadcast_to([P, NG, 3 * WIN]),
                                            ALU.mult).then_inc(s_ready, 1)
                    nc.gpsimd.tensor_copy(tst[:, s], qT_all[:, :, bass.ds(c0 + WIN, CH)]).then_inc(opnd_ready, 1)
                    nc.gpsimd.tensor_copy(hst[:, s], hT_all[:, bass.ds(c0, 3 * WIN)]).then_inc(opnd_ready, 1)
                    pool.wait_ge(s_ready, k + 1)
                    wait_alone(pool, pn_ready, k - 1)
                    nc.gpsimd.tensor_tensor(sqs[:, s], sst[:, s], win, ALU.mult).then_inc(opnd_ready, 1)

            steps(pool, step)

        @block.scalar
        def _(act):
            act.preload_act_table_set("natural_log_exp_and_others")
            act.wait_ge(c_in, 32)
            nc.scalar.activation(ec[:], c_sb[:], ACT.Exp, scale=-1.0).then_inc(ec_ready, 1)
            act.wait_ge(pmod_ready, 1)
            nc.scalar.activation(modT[:].rearrange("p j b -> p (j b)"), psC[:, 0:6 * NB], ACT.Copy).then_inc(modT_ready, 1)
            act.wait_ge(pmod_ready, 2)
            for j in range(2):
                nc.scalar.activation(modn[:, j * 384:(j + 1) * 384], psW[0:NB, j, 0:384], ACT.Copy).then_inc(modn_ready, 1)
            act.wait_ge(bias_set, 4)
            act.wait_ge(modT_ready, 2)
            act.wait_ge(con_in, 16)
            with act.Fori(0, NB) as b:
                for half in range(2):
                    n = 2 * b + half
                    act.wait_ge(mv_ready, 4 * n + 4)
                    nc.scalar.activation(rs_p[:, half], mv_p[:, half, :, 1], ACT.Ln, bias=bias[:, 0:1]).then_inc(lnv_p, 1)
                    act.wait_ge(lnv_p, n + 1)
                    nc.scalar.activation(rs_p[:, half], rs_p[:, half], ACT.Exp, scale=-0.5).then_inc(rs_ready, 1)
                    act.wait_ge(pT_ready, n + 1)
                    nc.scalar.activation(hT_all[:, bass.ds(b * TP + WIN + half * HALF, HALF)], psW[:, half], ACT.Identity,
                                         bias=modT[:, 0, bass.ds(b, 1)], scale=modT[:, 1, bass.ds(b, 1)]).then_inc(hT_ready, 1)
                    for g in range(NG):
                        act.wait_ge(pq_ready, 2 * n + g + 1)
                        nc.scalar.activation(qT_all[:, g, bass.ds(b * TP + WIN + half * HALF, HALF)], psD[:, 2 * half + g],
                                             ACT.Relu, bias=con[:, C_ROW + 2:C_ROW + 3],
                                             accum_out=qsum[:, g, half, bass.ds(b, 1)]).then_inc(q_ready, 1)
            act.wait_ge(pheb_ready, 2)
            for g in range(NG):
                nc.scalar.activation(selheb[:, g, 1], psX[:, 256 + g * 64:320 + g * 64], ACT.Copy).then_inc(selheb_ready, 1)
            act.wait_ge(pm1_ready, 1)
            nc.scalar.activation(h1[:], psX[0:64, 0:NB], ACT.Gelu, bias=b1_sb[:]).then_inc(h1_ready, 1)
            act.preload_act_table_set("natural_log_exp_and_others")
            act.wait_ge(z_ready, 1)
            nc.scalar.activation(sp[:, 1], sp[:, 0], ACT.Abs).then_inc(sp_act, 1)
            act.wait_ge(sp_act, 1)
            nc.scalar.activation(sp[:, 2], sp[:, 1], ACT.Exp, scale=-1.0).then_inc(sp_act, 1)
            act.wait_ge(sp_dve, 1)
            nc.scalar.activation(sp[:, 4], sp[:, 3], ACT.Ln).then_inc(sp_act, 1)
            act.wait_ge(p0_ready, 1)
            nc.scalar.activation(z8[:, 0:2].rearrange("p a b -> p (a b)"), psW[0:NB, 0, 0:256], ACT.Copy).then_inc(r0_act, 1)
            nc.scalar.activation(z8[:, 2], psW[0:NB, 0, 256:384], ACT.Relu).then_inc(r0_act, 1)
            act.wait_ge(r0_dve, 1)
            nc.scalar.activation(s8[:, 2], s8[:, 1], ACT.Ln).then_inc(r0_act, 1)
            act.wait_ge(r0_act, 3)
            nc.scalar.activation(s8[:, 3], s8[:, 2], ACT.Exp, scale=-0.5).then_inc(r0_act, 1)
            act.wait_ge(r0_dve, 4)
            nc.scalar.activation(s8[:, 7, 0:1], s8[:, 6, 1:2], ACT.Ln, bias=bias[0:NB, 0:1]).then_inc(r0_act, 1)
            act.wait_ge(r0_act, 5)
            nc.scalar.activation(s8[:, 7, 1:2], s8[:, 7, 0:1], ACT.Exp, scale=-0.5).then_inc(r0_act, 1)
            act.wait_ge(r0_dve, 7)
            nc.scalar.activation(s8[:, 11], s8[:, 8], ACT.Exp, bias=s8[:, 10, 0:1]).then_inc(r0_act, 1)

            def step(i, ph):
                k, s4 = i + 1, (ph + 1) % 4
                if there(i, 1):
                    e = ebuf[:, s4]
                    act.wait_ge(d2_ready, k + 1)
                    nc.scalar.activation(e, e, ACT.Ln, bias=bias[:, 1:2]).then_inc(ln_done, 1)
                    act.wait_ge(ln_done, 2 * k + 1)
                    nc.scalar.activation(e, e, ACT.Exp, scale=0.5).then_inc(ln_done, 1)
                    act.wait_ge(ln_done, 2 * k + 2)
                    nc.scalar.activation(e, e, ACT.Exp, scale=-1.0).then_inc(e_ready, 1)
                k, s = i - 1, (ph - 1) % 2
                if there(i, -1):
                    for w in range(2):
                        act.wait_ge(wt_ready, 8 * k + 4 * w + 4)
                        need(act, c_ready, k - 1)
                        nc.scalar.activation(wts[:, s, 4 * w:4 * w + 4].rearrange("p h t -> p (h t)"), psW[:, w],
                                             ACT.Copy).then_inc(wts_ready, 1)
                k, s = i - 2, ph % 2
                if there(i, -2):
                    b = k // CPB
                    act.wait_ge(pn2_ready, k + 1)
                    need(act, y_ready, k - 1)
                    nc.scalar.activation(h2T[:, s], pN2, ACT.Identity, bias=modT[:, 3, bass.ds(b, 1)],
                                         scale=modT[:, 4, bass.ds(b, 1)]).then_inc(h2T_ready, 1)
                k, s = i - 1, (ph - 1) % 2
                if there(i, -1):
                    act.wait_ge(c_ready, k + 1)
                    need(act, osp_ready, k - 1)
                    pc = pC.rearrange("p (h v e) -> p h v e", h=NH, v=2)
                    nc.scalar.activation(cst[0:WIN, s], pc[0:WIN, :, 0], ACT.Copy).then_inc(cst_ready, 1)
                    nc.scalar.activation(cst[WIN:P, s], pc[WIN:P, :, 1], ACT.Copy).then_inc(cst_ready, 1)
                    act.wait_ge(n2g_ready, 2 * (k + 1))
                    nc.scalar.activation(lnn[:], n2g[:, s], ACT.Ln).then_inc(lnn_done, 1)
                    act.wait_ge(lnn_done, k + 1)
                    need(act, osp_ready, k - 1)
                    nc.scalar.activation(rnn[:, s], lnn[:], ACT.Exp, scale=-0.5).then_inc(rnn_ready, 1)
                k, s = i + 3, (ph + 3) % 2
                if there(i, 3):
                    act.wait_ge(pn_ready, k + 1)
                    need(act, rows_in, 64 * (k - 1))
                    nc.scalar.activation(nst[:, s], pN, ACT.Copy).then_inc(nst_ready, 1)
                k, s4 = i + 2, (ph + 2) % 4
                if there(i, 2):
                    act.wait_ge(dist_ready, k + 1)
                    need(act, wsel_done, k - 3)
                    nc.scalar.activation(ebuf[:, s4].rearrange("p (r x) -> p r x", r=NR), dA, ACT.Relu).then_inc(amin_ready, 1)
                    need(act, c_ready, k - 3)
                    nc.scalar.activation(vst[:, s4, :, :, 0:HD], pV.rearrange("p (v h e) -> p h v e", v=2, h=NH),
                                         ACT.Relu).then_inc(vst_ready, 1)
                    need(act, osp_ready, k - 3)
                    nc.scalar.activation(qh[:, s4].rearrange("p a c -> p (a c)"), pQH, ACT.Copy).then_inc(qhs_ready, 1)
                k, s = i - 1, (ph - 1) % 2
                if there(i, -1):
                    act.wait_ge(po_ready, k + 1)
                    need(act, att_ready, k - 1)
                    nc.scalar.activation(oT[:, s], pO, ACT.Copy).then_inc(oT_ready, 1)
                    act.wait_ge(mvc_ready, k + 1)
                    nc.scalar.activation(lv_c[:], mv_c[:, s, 1:2], ACT.Ln, bias=bias[:, 0:1]).then_inc(lnc_done, 1)
                    act.wait_ge(lnc_done, k + 1)
                    need(act, nc_ready, k - 1)
                    nc.scalar.activation(rs_c[:, s:s + 1], lv_c[:], ACT.Exp, scale=-0.5).then_inc(rsc_ready, 1)

            steps(act, step)

        @block.vector
        def _(dve):
            n = [0]

            def link(ins):
                n[0] += 1
                ins.then_inc(dve_chain, 1)
                dve.wait_ge(dve_chain, n[0])

            v = nc.vector
            dve.wait_ge(ec_ready, 1)
            link(v.tensor_scalar(ec[:], ec[:], 1.0, None, ALU.add))
            link(v.reciprocal(ec[:], ec[:]))
            v.tensor_tensor(sil[:], c_sb[:], ec[:], ALU.mult).then_inc(sil_ready, 1)
            dve.wait_ge(modT_ready, 1)
            for j in (1, 4):
                last = v.tensor_scalar(modT[:, j], modT[:, j], 1.0, None, ALU.add)
            last.then_inc(modT_ready, 1)
            dve.wait_ge(modn_ready, 2)
            gview = modn[:].rearrange("b (u v d) -> b u v d", u=2, v=3)[:, :, 2]
            link(v.tensor_scalar(gsgn[:], gview, 0.0, 2.0, ALU.is_ge, ALU.mult))
            link(v.tensor_scalar(gabs[:], gview, -1.0, None, ALU.mult))
            link(v.tensor_tensor(gabs[:], gabs[:], gview, ALU.max))
            link(v.tensor_scalar(gabs[:], gabs[:], 0.25, None, ALU.max))
            v.scalar_tensor_tensor(out=gn[:], in0=gsgn[:], scalar=-1.0, in1=gabs[:], op0=ALU.add,
                                   op1=ALU.mult).then_inc(gates_n_ready, 1)
            dve.wait_ge(con_in, 16)
            for g in range(NG):
                v.tensor_copy(selheb[:, g, 0], con[:, C_SELQ:C_SELQ + NR * HD]).then_inc(selheb_ready, 1)

            with dve.Fori(0, NB) as b:
                for half in range(2):
                    n2b = 2 * b + half
                    dve.wait_ge(xp_in[half], 16 * b + 16)
                    for c in range(4):
                        v.bn_stats(st_p[:, half, c], xp[:, half, c]).then_inc(st_ready, 1)
                    for c in range(4):
                        wait_alone(dve, st_ready, 4 * n2b + c + 1)
                        v.bn_aggr(mv_p[:, half, c], st_p[:, half, c]).then_inc(mv_ready, 1)
                    dve.wait_ge(rs_ready, n2b + 1)
                    for c in range(4):
                        last = v.tensor_scalar(xn[:, half, c], xp[:, half, c], mv_p[:, half, c, 0:1],
                                               rs_p[:, half, c:c + 1], ALU.subtract, ALU.mult)
                    last.then_inc(xn_ready, 1)
                dve.wait_ge(q_ready, 4 * b + 4)
                v.tensor_reduce(qsum8[:, :, bass.ds(b, 1)], qT_all[:, :, bass.ds(b * TP + WIN, T // 8, step=8)],
                                AX_X, ALU.add).then_inc(qsum8_ready, 1)
            link(v.tensor_tensor(sig[:], qsum[:, :, 0], qsum[:, :, 1], ALU.add))
            link(v.tensor_scalar(sig[:], sig[:], 1.0 / T, None, ALU.mult))
            dve.wait_ge(qsum8_ready, NB)
            v.scalar_tensor_tensor(out=sig[:], in0=qsum8[:], scalar=0.5 * 8 / T, in1=sig[:], op0=ALU.mult,
                                   op1=ALU.add).then_inc(sig_ready, 1)
            dve.wait_ge(pm2_ready, 1)
            z = sp[:, 0].rearrange("p (g b) -> p g b", g=NG)
            for g in range(NG):
                link(v.tensor_scalar(z[:, g], psX[:, 64 + g * NB:64 + (g + 1) * NB], b2_sb[:, g:g + 1], 0.1, ALU.add, ALU.mult))
            for g in range(NG):
                last = v.tensor_scalar(z[:, g], z[:, g], base_sb[:, g:g + 1], None, ALU.add)
            last.then_inc(z_ready, 1)
            dve.wait_ge(sp_act, 2)
            v.tensor_scalar(sp[:, 3], sp[:, 2], 1.0, None, ALU.add).then_inc(sp_dve, 1)
            dve.wait_ge(sp_dve, 1)
            link(v.tensor_scalar(sp[:, 5], sp[:, 3], -1.0, None, ALU.add))
            link(v.tensor_scalar(sp[:, 6], sp[:, 5], 0.0, None, ALU.is_equal))
            link(v.tensor_tensor(sp[:, 5], sp[:, 5], sp[:, 6], ALU.add))
            link(v.reciprocal(sp[:, 5], sp[:, 5]))
            dve.wait_ge(sp_act, 3)
            link(v.tensor_tensor(sp[:, 6], sp[:, 6], sp[:, 4], ALU.add))
            link(v.tensor_tensor(sp[:, 6], sp[:, 6], sp[:, 5], ALU.mult))
            link(v.tensor_tensor(sp[:, 6], sp[:, 6], sp[:, 2], ALU.mult))
            link(v.scalar_tensor_tensor(out=sp[:, 7], in0=sp[:, 0], scalar=0.0, in1=sp[:, 6], op0=ALU.max, op1=ALU.add))
            v.tensor_scalar(aS[:].rearrange("p g b -> p (g b)"), sp[:, 7], con[:, C_ROW:C_ROW + 1],
                            con[:, C_ROW + 1:C_ROW + 2], ALU.mult, ALU.add).then_inc(aS_ready, 1)

            q0, hb0, v0 = z8[:, 0], z8[:, 1], z8[:, 2]
            h3 = "p (h e) -> p h e"
            dve.wait_ge(r0_act, 2)
            link(v.tensor_tensor(z8[:, 3], q0, q0, ALU.mult))
            link(v.tensor_reduce(s8[:, 0], z8[:, 3].rearrange(h3, h=NH), AX_X, ALU.add))
            v.tensor_scalar(s8[:, 1], s8[:, 0], 1e-18, None, ALU.max).then_inc(r0_dve, 1)
            link(v.tensor_scalar(s8[:, 4], s8[:, 0], GATE2, 0.1, ALU.is_gt, ALU.mult))
            dve.wait_ge(r0_act, 4)
            link(v.tensor_tensor(s8[:, 5], s8[:, 4], s8[:, 3], ALU.mult))
            link(v.tensor_tensor(z8[:, 4].rearrange(h3, h=NH), hb0.rearrange(h3, h=NH),
                                 s8[:, 5].unsqueeze(2).broadcast_to([NB, NH, HD]), ALU.mult))
            total = TOPK * float(np.exp(-np.sqrt(1e-8)))
            link(v.scalar_tensor_tensor(out=z8[:, 5], in0=v0, scalar=total / (total + 1e-8), in1=z8[:, 4],
                                        op0=ALU.mult, op1=ALU.add))
            v.tensor_tensor(z8[:, 6], z8[:, 5], q0, ALU.mult).then_inc(r0_dve, 1)
            dve.wait_ge(r0_pe, 1)
            v.tensor_copy(o0T[:], psX[:, 128:128 + NB]).then_inc(r0_dve, 1)
            dve.wait_ge(r0_pe, 2)
            link(v.tensor_tensor(z8[:, 7], psX[0:NB, 256:384], gn[:, 0], ALU.mult))
            link(v.tensor_tensor(z8[:, 7], z8[:, 7], x0_sb[:], ALU.add))
            link(v.bn_stats(s8[:, 9, 0:6], z8[:, 7]))
            v.bn_aggr(s8[:, 6, 0:2], s8[:, 9, 0:6]).then_inc(r0_dve, 1)
            dve.wait_ge(r0_act, 6)
            v.tensor_scalar(z8[:, 8], z8[:, 7], s8[:, 6, 0:1], s8[:, 7, 1:2], ALU.subtract, ALU.mult).then_inc(r0_dve, 1)
            dve.wait_ge(r0_pe, 3)
            link(v.tensor_tensor(h0T[:], psX[:, 136:136 + NB], modT[:, 4], ALU.mult))
            v.tensor_tensor(h0T[:], h0T[:], modT[:, 3], ALU.add).then_inc(r0_dve, 1)
            dve.wait_ge(r0_pe, 4)
            lg = s8[:, 8]
            link(v.tensor_copy(lg, psX[0:NB, 144:144 + NE]))
            link(v.max(s8[:, 9], lg))
            v.tensor_scalar(s8[:, 10, 0:1], s8[:, 9, 0:1], -1.0, None, ALU.mult).then_inc(r0_dve, 1)
            link(v.tensor_scalar(s8[:, 12], lg, s8[:, 9, 1:2], None, ALU.is_gt))
            link(v.tensor_scalar(s8[:, 13], lg, s8[:, 9, 1:2], None, ALU.is_equal))
            link(v.tensor_copy(s8[:, 14], s8[:, 13]))
            for sh in (1, 2, 4):
                link(v.tensor_copy(s8[:, 15], s8[:, 14]))
                link(v.tensor_tensor(s8[:, 14, sh:NE], s8[:, 14, sh:NE], s8[:, 15, 0:NE - sh], ALU.add))
            link(v.tensor_reduce(s8[:, 16, 0:1], s8[:, 12], AX_X, ALU.add))
            link(v.tensor_scalar(s8[:, 16, 1:2], s8[:, 16, 0:1], -1.0, 2.0, ALU.mult, ALU.add))
            link(v.tensor_scalar(s8[:, 17], s8[:, 14], s8[:, 16, 1:2], None, ALU.is_le))
            link(v.tensor_tensor(s8[:, 17], s8[:, 17], s8[:, 13], ALU.mult))
            link(v.tensor_tensor(s8[:, 17], s8[:, 17], s8[:, 12], ALU.add))
            dve.wait_ge(r0_act, 7)
            link(v.tensor_tensor(s8[:, 18], s8[:, 11], s8[:, 17], ALU.mult))
            link(v.tensor_reduce(s8[:, 19, 0:1], s8[:, 18], AX_X, ALU.add))
            link(v.reciprocal(s8[:, 19, 1:2], s8[:, 19, 0:1]))
            v.tensor_scalar(s8[:, 20], s8[:, 18], s8[:, 19, 1:2], None, ALU.mult).then_inc(r0_dve, 1)
            dve.wait_ge(r0_pe, 5)
            v.tensor_copy(gateT[:], psX[0:NE, 152:152 + NB]).then_inc(r0_dve, 1)
            dve.wait_ge(r0_pe, 6)
            link(v.tensor_copy(gate_er[:].rearrange("p k b -> p (k b)"), psX[:, 160:160 + 4 * NB]))
            for kt in range(4):
                v.tensor_tensor(bsc[:, kt], b_sb[:, kt].unsqueeze(1).broadcast_to([P, NB, D]),
                                gate_er[:, kt].unsqueeze(2).broadcast_to([P, NB, D]), ALU.mult).then_inc(bsc_ready, 1)
            for pr in range(NB // 2):
                dve.wait_ge(pgate_ready, pr + 1)
                gate_ps = psC[:, :].rearrange("p (b u d) -> p b u d", b=2, u=2)
                link(v.tensor_copy(gaw[:], gate_ps))
                v.tensor_tensor(dec_b[:, 2 * pr:2 * pr + 2], dec_sb[:].unsqueeze(1).broadcast_to([P, 2, D]), gaw[:, :, 0],
                                ALU.mult).then_inc(decb_ready, 1)
                dve.wait_ge(pG_ready, pr + 1)
                pg = psX[:, 0:2 * D].rearrange("p (b d) -> p b d", b=2)
                link(v.tensor_tensor(g_b[:, 2 * pr:2 * pr + 2], pg, ident.unsqueeze(1).broadcast_to([P, 2, D]), ALU.add))
                link(v.tensor_tensor(g_b[:, 2 * pr:2 * pr + 2], g_b[:, 2 * pr:2 * pr + 2], gaw[:, :, 1], ALU.mult))
                v.tensor_scalar(bias[0:1, 3:4], bias[0:1, 3:4], 0.0, None, ALU.mult).then_inc(gb_ready, 1)

            def step(i, ph):
                k, s4 = i + 1, (ph + 1) % 4
                if there(i, 1):
                    dve.wait_ge(qhs_ready, k + 1)
                    e = ebuf[:, s4].rearrange("p (r x) -> p r x", r=NR)
                    v.scalar_tensor_tensor(out=e, in0=dB, scalar=0.0, in1=e, op0=ALU.max, op1=ALU.min).then_inc(d2_ready, 1)

                def rounds(rnd):
                    k, s, s4 = i, ph % 2, ph % 4
                    src = ebuf[:, s4] if rnd == 0 else work[:, s]
                    for half in range(2):
                        wait_alone(dve, picked, 16 * k + 4 * (rnd - 1) + 3 + half)
                        for h in range(4 * half, 4 * half + 4):
                            last = v.max(m8[:, h], src[:, h * WIN:(h + 1) * WIN])
                        last.then_inc(picked, 1)
                    for half in range(2):
                        wait_alone(dve, picked, 16 * k + 4 * rnd + 1 + half)
                        for h in range(4 * half, 4 * half + 4):
                            cols = slice(h * WIN, (h + 1) * WIN)
                            last = v.match_replace(work[:, s, cols], m8[:, h], src[:, cols], 0.0)
                        last.then_inc(picked, 1)

                if there(i, 0):
                    dve.wait_ge(e_ready, i + 1)
                    wait_alone(dve, wsel_done, i - 1)
                    rounds(0)
                k, s = i - 2, ph % 2
                if there(i, -2):
                    dve.wait_ge(rsc_ready, k + 1)
                    need(dve, pn2_ready, k - 1)
                    v.tensor_scalar(n_c[:, s], x2[:, s], mv_c[:, s, 0:1], rs_c[:, s:s + 1], ALU.subtract,
                                    ALU.mult).then_inc(nc_ready, 1)
                k, s = i - 1, (ph - 1) % 2
                if there(i, -1):
                    dve.wait_ge(qsq_ready, k + 1)
                    need(dve, n2g_ready, 2 * (k - 1))
                    v.tensor_reduce(n2[:, s], qsq[:].rearrange("p (h e) -> p h e", h=NH), AX_X, ALU.add).then_inc(n2_ready, 1)
                if there(i, 0):
                    rounds(1)
                if there(i, -1):
                    dve.wait_ge(cst_ready, 2 * (k + 1))
                    need(dve, rden_ready, k - 1)
                    v.tensor_scalar(den[:, s], cst[:, s, :, HD], 1e-8, None, ALU.add).then_inc(den_done, 1)
                    dve.wait_ge(den_done, k + 1)
                    need(dve, osp_ready, k - 1)
                    v.reciprocal(rden[:, s], den[:, s]).then_inc(rden_ready, 1)
                if there(i, 0):
                    rounds(2)
                if there(i, -1):
                    dve.wait_ge(att_ready, k + 1)
                    dve.wait_ge(xs_in[(ph - 1) % 4], 16 * (k // 4) + 16)
                    v.tensor_tensor(x2[:, s], pAtt, xs[:, (ph - 1) % 4], ALU.add).then_inc(x2_ready, 1)
                    dve.wait_ge(x2_ready, k + 1)
                    v.bn_stats(st_c[:], x2[:, s]).then_inc(stc_ready, 1)
                    wait_alone(dve, stc_ready, k + 1)
                    v.bn_aggr(mv_c[:, s], st_c[:]).then_inc(mvc_ready, 1)
                k, s = i - 2, ph % 2
                if there(i, 0):
                    rounds(3)
                if there(i, -2):
                    dve.wait_ge(y_ready, k + 1)
                    need(dve, out_in[s], 16 * ((k - 2) // 2) + 16 if isinstance(k, int) else 16 * (k // 2))
                    v.tensor_tensor(yo[:, s], pY, x2[:, s], ALU.add).then_inc(yo_ready, 1)

            steps(dve, step)

        @block.tensor
        def _(pe):
            mm = nc.tensor.matmul
            pe.wait_ge(sil_ready, 1)
            for j in range(6):
                last = mm(psC[:, j * NB:(j + 1) * NB], wmod_sb[:, j * D:(j + 1) * D], sil[:], start=True, stop=True)
            last.then_inc(pmod_ready, 1)
            for j in range(2):
                last = mm(psW[0:NB, j, 0:384], sil[:], wmod_sb[:, j * 384:(j + 1) * 384], start=True, stop=True)
            last.then_inc(pmod_ready, 1)
            pe.wait_ge(con_in, 16)
            pe.wait_ge(diag_ready, 2 * NG)
            for g in range(NG):
                mm(psX[:, 256 + g * 64:320 + g * 64], udiag[:, g].rearrange("k r e -> k (r e)"),
                   vdiag[:, g].rearrange("k r e -> k (r e)"), start=True, stop=True).then_inc(pheb_ready, 1)
            pe.wait_ge(wq_in, 16)
            pe.wait_ge(modn_ready, 2)
            with pe.Fori(0, NB) as b:
                for half in range(2):
                    n = 2 * b + half
                    pe.wait_ge(xn_ready, n + 1)
                    if half == 1:
                        pe.wait_ge(hT_ready, n)
                    for c in range(4):
                        last = nc.tensor.transpose(psW[:, half, c * P:(c + 1) * P], xn[:, half, c], ident)
                    last.then_inc(pT_ready, 1)
                    pe.wait_ge(hT_ready, n + 1)
                    for g in range(NG):
                        mm(psD[:, 2 * half + g], encq_sb[:, g], hT_all[:, bass.ds(b * TP + WIN + half * HALF, HALF)],
                           start=True, stop=True).then_inc(pq_ready, 1)
            pe.wait_ge(wts_in, 16 * 13)
            pe.wait_ge(sig_ready, 1)
            pe.wait_ge(selheb_ready, 2 * NG)
            for g in range(NG):
                last = mm(psX[0:64, 0:NB], w1_sb[:, g], sig[:, g], start=(g == 0), stop=(g == NG - 1))
            last.then_inc(pm1_ready, 1)
            pe.wait_ge(h1_ready, 1)
            for g in range(NG):
                last = mm(psX[:, 64 + g * NB:64 + (g + 1) * NB], w2_sb[:, g], h1[:], start=True, stop=True)
            last.then_inc(pm2_ready, 1)
            pe.wait_ge(selheb_ready, 2 * NG)
            first = slice(WIN, NB * TP, TP)
            for g in range(NG):
                o = psW[0:NB, 0, 0:256].rearrange("p (a r g e) -> p a r g e", a=2, r=NR, g=NG)[:, :, :, g]
                mm(o, qT_all[:, g, first], selheb[:, g].rearrange("p a (r e) -> p a r e", r=NR), start=True, stop=True)
            mm(psW[0:NB, 0, 256:384], hT_all[:, first], encv_sb[:], start=True, stop=True).then_inc(p0_ready, 1)
            pe.wait_ge(r0_dve, 2)
            nc.tensor.transpose(psX[:, 128:128 + NB], z8[:, 6], con[0:NB, 0:NB]).then_inc(r0_pe, 1)
            pe.wait_ge(r0_dve, 3)
            mm(psX[0:NB, 256:384], o0T[:], dec_sb[:], start=True, stop=True).then_inc(r0_pe, 1)
            pe.wait_ge(r0_dve, 5)
            nc.tensor.transpose(psX[:, 136:136 + NB], z8[:, 8], con[0:NB, 0:NB]).then_inc(r0_pe, 1)
            pe.wait_ge(r0_dve, 6)
            mm(psX[0:NB, 144:144 + NE], h0T[:], wr_sb[:], start=True, stop=True).then_inc(r0_pe, 1)
            pe.wait_ge(r0_dve, 8)
            nc.tensor.transpose(psX[0:NE, 152:152 + NB], s8[:, 20], con[0:NB, 0:NB]).then_inc(r0_pe, 1)
            pe.wait_ge(r0_dve, 9)
            for kt in range(4):
                last = mm(psX[:, 160 + kt * NB:160 + (kt + 1) * NB], con[0:NE, C_EXP + kt * P:C_EXP + (kt + 1) * P], gateT[:],
                          start=True, stop=True)
            last.then_inc(r0_pe, 1)
            pe.wait_ge(gates_n_ready, 1)
            pe.wait_ge(bsc_ready, 4)
            for pr in range(NB // 2):
                need(pe, gb_ready, pr)
                for j in range(2):
                    last = mm(psC[:, j * 256:(j + 1) * 256], con[0:NB, 2 * pr + j:2 * pr + j + 1].broadcast_to([NB, P]),
                              gn[:].rearrange("b u d -> b (u d)"), start=True, stop=True)
                last.then_inc(pgate_ready, 1)
                for kt in range(4):
                    last = mm(psX[:, 0:2 * D], a_sb[:, kt], bsc[:, kt, 2 * pr:2 * pr + 2].rearrange("p b d -> p (b d)"),
                              start=(kt == 0), stop=(kt == 3))
                last.then_inc(pG_ready, 1)
            pe.wait_ge(bf_set, 2)
            pe.wait_ge(gb_ready, NB // 2)

            def step(i, ph):
                k, s, s4 = i - 1, (ph - 1) % 2, (ph - 1) % 4
                if there(i, -1):
                    pe.wait_ge(w_ready, k + 1)
                    need(pe, nst_ready, min(k + 4, NCH) if isinstance(k, int) else k + 4)
                    for h in range(NH):
                        if h % 4 == 0:
                            need(pe, wts_ready, 2 * k - 1 + h // 4)
                        nc.tensor.transpose(psW[:, h // 4, (h % 4) * P:(h % 4 + 1) * P], wun[:, s, h],
                                            ident).then_inc(wt_ready, 1)
                k2, s2 = i + 2, (ph + 2) % 2
                if there(i, 2):
                    k = k2
                    pe.wait_ge(rows_in, 64 * (k + 1))
                    need(pe, d2_ready, k)
                    for r in range(NR):
                        mm(psD[:, r, 0:4 * WIN], ident_bf[:], mask_bf[:], start=True, stop=False, skip_group_check=True)
                    for g in range(NG):
                        for r in range(NR):
                            row = slice(32 * r, 32 * r + HD + 2)
                            ca, cb = g * WIN, 2 * WIN + g * WIN
                            mm(psD[:, r, ca:ca + WIN], tst[row, s2, g], sst[row, s2, g, WIN:2 * WIN],
                               start=False, stop=False, skip_group_check=True)
                            mm(psD[0:WIN, r, cb:cb + WIN], tst[row, s2, g, 0:WIN], sst[row, s2, g, 0:WIN],
                               start=False, stop=False, skip_group_check=True)
                            mm(psD[WIN:P, r, cb:cb + WIN], tst[row, s2, g, WIN:CH], sst[row, s2, g, 2 * WIN:3 * WIN],
                               start=False, stop=(g == NG - 1), skip_group_check=True)
                    mm(pV[:, P:2 * P], hst[:, s2, WIN:3 * WIN], encv_sb[:], start=True, stop=True)
                    mm(pV[0:WIN, 0:P], hst[:, s2, WIN:2 * WIN], encv_sb[:], start=True, stop=True)
                    mm(pV[WIN:P, 0:P], hst[:, s2, 0:WIN], encv_sb[:], start=True, stop=True)
                    for g in range(NG):
                        o = pQH.rearrange("p (a r g e) -> p a r g e", a=2, r=NR, g=NG)[:, :, :, g]
                        last = mm(o, tst[:, s2, g], selheb[:, g].rearrange("p a (r e) -> p a r e", r=NR),
                                  start=True, stop=True)
                    last.then_inc(dist_ready, 1)
                k = i - 1
                if there(i, -1):
                    need(pe, x2_ready, k)
                    pe.wait_ge(vst_ready, k + 1)
                    for h in range(NH):
                        if h % 4 == 0:
                            pe.wait_ge(wts_ready, 2 * k + 1 + h // 4)
                        last = mm(pC[:, h * 2 * VD:(h + 1) * 2 * VD], wts[:, s, h],
                                  vst[:, s4, h].rearrange("p v e -> p (v e)"), start=True, stop=True)
                    last.then_inc(c_ready, 1)
                k, s = i - 2, ph % 2
                if there(i, -2):
                    pe.wait_ge(nc_ready, k + 1)
                    need(pe, yo_ready, k)
                    nc.tensor.transpose(pN2, n_c[:, s], ident).then_inc(pn2_ready, 1)
                k, s = i + 3, (ph + 3) % 2
                if there(i, 3):
                    pe.wait_ge(opnd_ready, 3 * (k + 1))
                    need(pe, nst_ready, k)
                    for g in range(NG):
                        last = mm(pN, seln[:, g], sqs[:, s, g], start=(g == 0), stop=(g == NG - 1))
                    last.then_inc(pn_ready, 1)
                k, s = i - 1, (ph - 1) % 2
                if there(i, -1):
                    pe.wait_ge(osp_ready, k + 1)
                    nc.tensor.transpose(pO, osp[:, s], ident).then_inc(po_ready, 1)
                    pe.wait_ge(oT_ready, k + 1)
                    mm(pAtt, oT[:, s], dec_b[:, bass.ds(k // CPB, 1)].squeeze(1), start=True, stop=True).then_inc(att_ready, 1)
                k, s = i - 2, ph % 2
                if there(i, -2):
                    pe.wait_ge(h2T_ready, k + 1)
                    mm(pY, h2T[:, s], g_b[:, bass.ds(k // CPB, 1)].squeeze(1), start=True, stop=True).then_inc(y_ready, 1)

            steps(pe, step)


def kernel(**inputs):
    import concourse.bacc as bacc
    from concourse.bass_utils import run_bass_kernel_spmd

    a = {k.replace("L0_", ""): np.asarray(v) for k, v in inputs.items()}

    def padded(w):
        w = w.reshape(w.shape[:-1] + (NR, NG, HD))
        w = np.moveaxis(w, -2, -3)
        w = np.pad(w, [(0, 0)] * (w.ndim - 1) + [(0, 32 - HD)])
        return w.reshape(w.shape[:-3] + (NG, P))

    encq = a["attn_enc_q"].transpose(1, 0, 2).reshape(D, P)
    arrays = {
        "x": a["attn_x"].reshape(NB * T, D),
        "encq": padded(encq),
        "encv": a["attn_enc_v"].transpose(1, 0, 2).reshape(D, P),
        "w1": padded(a["attn_metric_w1"].T).transpose(2, 1, 0),
        "b1": a["attn_metric_b1"].reshape(64, 1),
        "w2": padded(a["attn_metric_w2"]),
        "b2": padded(a["attn_metric_b2"]).T,
        "base": padded(a["attn_base_metric"].reshape(P)).T,
        "hebu": a["attn_hebb_U"].transpose(0, 2, 1).reshape(NH * RANK, HD),
        "hebv": a["attn_hebb_V"].reshape(NH * RANK, HD),
        "dec": a["attn_decoder"],
        "wr": a["ffn_Wr"].T,
        "amat": a["ffn_A"].reshape(4, P, D).transpose(1, 0, 2),
        "bmat": a["ffn_Bw"].transpose(0, 2, 1).reshape(4, P, D).transpose(1, 0, 2),
        "cin": a["c"].T,
        "wmod": a["wmod"],
        "consts": constants(),
    }
    nc = bacc.Bacc("TRN2", target_bir_lowering=False, num_devices=1)
    arrays = {f"in_{k}": np.ascontiguousarray(v) for k, v in arrays.items()}
    args = [nc.dram_tensor(k, v.shape, F32, kind="ExternalInput").ap() for k, v in arrays.items()]
    args.append(nc.dram_tensor("out_0", (NB * T, D), F32, kind="ExternalOutput").ap())
    adaln_block(nc, *args)
    r = run_bass_kernel_spmd(nc, [arrays], core_ids=[0])
    return r.results[0]["out_0"].reshape(NB, T, D)
```

```python
from contextlib import ExitStack

import numpy as np

import concourse.bass as bass
from concourse import mybir

ALU = mybir.AluOpType
ACT = mybir.ActivationFunctionType
F32 = mybir.dt.float32
BF16 = mybir.dt.bfloat16
AX_X = mybir.AxisListType.X

P = 128
NB, T, D = 8, 1024, 128
NH, HD = 8, 16
WIN, TOPK = 64, 32
RANK = 4
NE, ER = 8, 64
NR, NG = 4, 2
TP = T + WIN
CH = P
NCH = NB * T // CH
CPB = T // CH
HALF = 512
VD = HD + 1
BIG = 1e30
GONE = -1e4
EPS_LN = 1e-5
GATE2 = 0.2 * 0.2

C_ID = 0
C_MASK = C_ID + P
C_UNF = C_MASK + 4 * WIN
C_ROW = C_UNF + 2 * WIN
C_SELN = C_ROW + 3
C_SELQ = C_SELN + NG * NH
C_BLK = C_SELQ + NR * HD
C_EXP = C_BLK + NG * NR
C_END = C_EXP + NE * ER


def constants():
    c = np.zeros((P, C_END), np.float32)
    c[:, C_ID:C_ID + P] = np.eye(P, dtype=np.float32)
    i = (np.arange(P) % WIN)[:, None]
    late = (np.arange(P) >= WIN)[:, None]
    j = np.arange(WIN)[None, :]
    own = np.where(j > i, BIG, np.where(j == i, -BIG, 0.0))
    before = np.where(j > i, 0.0, BIG)
    a = np.where(late, before, own)
    b = np.where(late, own, before)
    c[:, C_MASK:C_MASK + 4 * WIN] = np.concatenate([a, a, b, b], 1)
    c[:, C_UNF:C_UNF + 2 * WIN] = np.concatenate([a, b], 1) <= 0
    e = np.arange(P) % 32
    r = np.arange(P) // 32
    c[:, C_ROW] = np.where(e < HD, -2.0, 0.0)
    c[:, C_ROW + 1] = e == HD + 1
    c[:, C_ROW + 2] = (e == HD) | (e == HD + 1)
    for p in range(P):
        if e[p] < HD:
            for g in range(NG):
                c[p, C_SELN + g * NH + NG * r[p] + g] = -0.5
            c[p, C_SELQ + r[p] * HD + e[p]] = 1.0
    for h in range(NH):
        c[h * RANK:(h + 1) * RANK, C_BLK + (h % NG) * NR + h // NG] = 1.0
    for x in range(NE):
        c[x, C_EXP + x * ER:C_EXP + (x + 1) * ER] = 1.0
    return c


def adaln_block(nc, x, encq, encv, w1, b1, w2, b2, base, hebu, hebv, dec, wr, amat, bmat, cin, wmod, consts, out):
    ctx = ExitStack()

    def sb(name, shape, dt=F32):
        return ctx.enter_context(nc.sbuf_tensor(name, shape, dt))

    def sem(name):
        return ctx.enter_context(nc.semaphore(name))

    with ctx:
        con = sb("con", [P, C_END])
        encq_sb = sb("encq_sb", [P, NG, P])
        encv_sb = sb("encv_sb", [P, P])
        w1_sb = sb("w1_sb", [P, NG, 64])
        b1_sb = sb("b1_sb", [64, 1])
        w2_sb = sb("w2_sb", [64, NG, P])
        b2_sb = sb("b2_sb", [P, NG])
        base_sb = sb("base_sb", [P, NG])
        hebu_sb = sb("hebu_sb", [NH * RANK, HD])
        hebv_sb = sb("hebv_sb", [NH * RANK, HD])
        dec_sb = sb("dec_sb", [P, D])
        wr_sb = sb("wr_sb", [P, NE])
        a_sb = sb("a_sb", [P, 4, D])
        b_sb = sb("b_sb", [P, 4, D])
        c_sb = sb("c_sb", [P, NB])
        wmod_sb = sb("wmod_sb", [P, 6 * D])
        x0_sb = sb("x0_sb", [NB, D])
        ident = con[:, C_ID:C_ID + P]
        seln = con[:, C_SELN:C_SELN + NG * NH].rearrange("p (g h) -> p g h", g=NG)
        unf = con[:, C_UNF:C_UNF + 2 * WIN].rearrange("p (v j) -> p v j", v=2)
        ident_bf = sb("ident_bf", [P, P], BF16)
        mask_bf = sb("mask_bf", [P, 4 * WIN], BF16)
        bias = sb("bias", [P, 4])
        hT_all = sb("hT_all", [P, NB * TP])
        qT_all = sb("qT_all", [P, NG, NB * TP])
        dec_b = sb("dec_b", [P, NB, D])
        g_b = sb("g_b", [P, NB, D])
        selheb = sb("selheb", [P, NG, 2, NR * HD])
        aS = sb("aS", [P, NG, NB])
        modT = sb("modT", [P, 6, NB])
        ec = sb("ec", [P, NB])
        sil = sb("sil", [P, NB])
        modn = sb("modn", [NB, 6 * D])
        gn = sb("gn", [NB, 2, D])
        gsgn = sb("gsgn", [NB, 2, D])
        gabs = sb("gabs", [NB, 2, D])
        udiag = sb("udiag", [NH * RANK, NG, NR, 32])
        vdiag = sb("vdiag", [NH * RANK, NG, NR, HD])
        key = sb("key", [P, 2, NH * WIN])
        big = sb("big", [P, 2, 2, NH * CH])
        xp = big[:, 0].rearrange("p s (u c d) -> p (s u) c d", u=2, c=4)
        xn = key[:].rearrange("p h (c d) -> p h c d", c=4)
        st_p = sb("st_p", [P, 4, 4, 6])
        mv_p = sb("mv_p", [P, 4, 4, 2])
        rs_p = sb("rs_p", [P, 4, 4])
        qsum = sb("qsum", [P, NG, 2, NB])
        qsum8 = sb("qsum8", [P, NG, NB])
        sig = sb("sig", [P, NG, NB])
        h1 = sb("h1", [64, NB])
        sp = sb("sp", [P, 8, NG * NB])
        z8 = sb("z8", [NB, 9, P])
        s8 = sb("s8", [NB, 24, 8])
        o0T = sb("o0T", [P, NB])
        h0T = sb("h0T", [P, NB])
        gateT = sb("gateT", [NE, NB])
        mI = sb("mI", [P, 4, D])
        gate_er = sb("gate_er", [P, 4, NB])
        bsc = big[:].rearrange("p a s (b d) -> p (a s) b d", b=NB)
        hst = sb("hst", [P, 2, 3 * WIN])
        tst = sb("tst", [P, 2, NG, CH])
        sst = sb("sst", [P, 2, NG, 3 * WIN])
        sqs = sb("sqs", [P, 2, NG, 3 * WIN])
        nst = sb("nst", [NH, 2, 3 * WIN])
        work = sb("work", [P, 2, NH * WIN])
        m8 = sb("m8", [P, NH, 8])
        wun = big[:, 0].rearrange("p s (h j) -> p s h j", h=NH)
        wts = big[:, 1].rearrange("p s (h t) -> p s h t", h=NH)
        vst = sb("vst", [P, 4, NH, 2, VD])
        qh = sb("qh", [P, 4, 2, P])
        cst = sb("cst", [P, 2, NH, VD])
        den = sb("den", [P, 2, NH])
        rden = sb("rden", [P, 2, NH])
        qsq = sb("qsq", [P, NH * HD])
        n2 = sb("n2", [P, 2, NH])
        n2g = sb("n2g", [P, 2, NH])
        lnn = sb("lnn", [P, NH])
        rnn = sb("rnn", [P, 2, NH])
        gat = sb("gat", [P, 2, NH])
        hsc = sb("hsc", [P, NH])
        t1 = sb("t1", [P, NH * HD])
        t2 = sb("t2", [P, NH * HD])
        osp = sb("osp", [P, 2, NH * HD])
        oT = sb("oT", [P, 2, CH])
        xs = sb("xs", [P, 4, D])
        x2 = sb("x2", [P, 2, D])
        st_c = sb("st_c", [P, 6])
        mv_c = sb("mv_c", [P, 2, 2])
        lv_c = sb("lv_c", [P, 1])
        rs_c = sb("rs_c", [P, 2])
        n_c = sb("n_c", [P, 2, D])
        h2T = sb("h2T", [P, 2, CH])
        yo = sb("yo", [P, 2, D])

        psD = ctx.enter_context(nc.psum_tensor("psD", [P, 4, 512], F32))
        psW = ctx.enter_context(nc.psum_tensor("psW", [P, 2, 512], F32))
        psC = ctx.enter_context(nc.psum_tensor("psC", [P, 512], F32))
        psX = ctx.enter_context(nc.psum_tensor("psX", [P, 512], F32))
        dA = psD[:, :, 0:2 * WIN]
        dB = psD[:, :, 2 * WIN:4 * WIN]
        pV = psD[:, 0, 256:512]
        pQH = psD[:, 1, 256:512]
        pC = psC[:, 0:NH * 2 * VD]
        pO = psX[:, 2 * P:3 * P]
        pAtt = psX[:, 3 * P:4 * P]
        pN2 = psX[:, 0:P]
        pY = psX[:, P:2 * P]
        pN = psW[0:NH, 0, 0:3 * WIN]

        con_in = sem("con_in")
        c_in = sem("c_in")
        wq_in = sem("wq_in")
        wts_in = sem("wts_in")
        bias_set = sem("bias_set")
        bf_set = sem("bf_set")
        ec_ready = sem("ec_ready")
        sil_ready = sem("sil_ready")
        pmod_ready = sem("pmod_ready")
        modT_ready = sem("modT_ready")
        modn_ready = sem("modn_ready")
        dve_chain = sem("dve_chain")
        pool_chain = sem("pool_chain")
        gates_n_ready = sem("gates_n_ready")
        pgate_ready = sem("pgate_ready")
        gaw_ready = sem("gaw_ready")
        decb_ready = sem("decb_ready")
        diag_ready = sem("diag_ready")
        pheb_ready = sem("pheb_ready")
        selheb_ready = sem("selheb_ready")
        xp_in = [sem(f"xp_in{i}") for i in range(4)]
        mv_ready = sem("mv_ready")
        lnv_p = sem("lnv_p")
        rs_ready = sem("rs_ready")
        st_ready = sem("st_ready")
        xn_ready = sem("xn_ready")
        pT_ready = sem("pT_ready")
        hT_ready = sem("hT_ready")
        pq_ready = sem("pq_ready")
        q_ready = sem("q_ready")
        qsum8_ready = sem("qsum8_ready")
        pads_ready = sem("pads_ready")
        sig_ready = sem("sig_ready")
        pm1_ready = sem("pm1_ready")
        h1_ready = sem("h1_ready")
        pm2_ready = sem("pm2_ready")
        z_ready = sem("z_ready")
        sp_act = sem("sp_act")
        sp_dve = sem("sp_dve")
        aS_ready = sem("aS_ready")
        p0_ready = sem("p0_ready")
        r0_act = sem("r0_act")
        r0_dve = sem("r0_dve")
        r0_pe = sem("r0_pe")
        gb_free = sem("gb_free")
        bsc_ready = sem("bsc_ready")
        pG_ready = sem("pG_ready")
        gatew_ready = sem("gatew_ready")
        gb_ready = sem("gb_ready")
        ones_set = sem("ones_set")
        waits_alone = sem("waits_alone")
        opnd_ready = sem("opnd_ready")
        s_ready = sem("s_ready")
        pn_ready = sem("pn_ready")
        nst_ready = sem("nst_ready")
        rows_in = [sem("rows_in0"), sem("rows_in1")]
        dist_ready = sem("dist_ready")
        amin_ready = sem("amin_ready")
        d2_ready = sem("d2_ready")
        ln_done = sem("ln_done")
        key_ready = sem("key_ready")
        vst_ready = sem("vst_ready")
        qhs_ready = sem("qhs_ready")
        picked = sem("picked")
        square_done = sem("square_done")
        wsel_ready = sem("wsel_ready")
        w_ready = sem("w_ready")
        wt_ready = sem("wt_ready")
        wts_ready = sem("wts_ready")
        c_ready = sem("c_ready")
        cst_ready = sem("cst_ready")
        den_done = sem("den_done")
        rden_ready = sem("rden_ready")
        qsq_ready = sem("qsq_ready")
        n2_ready = sem("n2_ready")
        n2g_ready = sem("n2g_ready")
        lnn_done = sem("lnn_done")
        rnn_ready = sem("rnn_ready")
        mix_step = sem("mix_step")
        osp_ready = sem("osp_ready")
        po_ready = sem("po_ready")
        oT_ready = sem("oT_ready")
        att_ready = sem("att_ready")
        xs_in = [sem(f"xs_in{i}") for i in range(4)]
        x2_ready = sem("x2_ready")
        stc_ready = sem("stc_ready")
        mvc_ready = sem("mvc_ready")
        lnc_done = sem("lnc_done")
        rsc_ready = sem("rsc_ready")
        nc_ready = sem("nc_ready")
        pn2_ready = sem("pn2_ready")
        h2T_ready = sem("h2T_ready")
        y_ready = sem("y_ready")
        yo_ready = sem("yo_ready")
        out_in = [sem("out_in0"), sem("out_in1")]

        def need(eng, s, value):
            if isinstance(value, int) and value <= 0:
                return
            eng.wait_ge(s, value)

        def wait_alone(eng, s, value):
            if isinstance(value, int) and value <= 0:
                return
            eng.wait_ge(s, value)
            if not isinstance(value, int):
                eng.sem_inc(waits_alone, 1)

        FIRST, LAST = -3, NCH + 2
        LOOP0, LOOP1, UNROLL = 5, 58, 4

        def steps(eng, step, routing=None):
            for i in range(FIRST, LOOP0):
                if routing and i <= 1:
                    routing(i)
                step(i, i % UNROLL)
            with eng.Fori(LOOP0, LOOP1, UNROLL) as i0:
                for u in range(UNROLL):
                    step(i0 + u, (LOOP0 + u) % UNROLL)
            for i in range(LOOP1 + UNROLL - 1, LAST + 1):
                step(i, i % UNROLL)

        def there(i, off):
            return not isinstance(i, int) or 0 <= i + off < NCH

        def column(k):
            return k * CH + (k // CPB) * WIN

        block = ctx.enter_context(nc.Block())

        @block.sync
        def _(sync):
            xh = x.rearrange("(n c p) d -> p n c d", c=4, p=P)
            for n in range(2):
                sync.dma_start(xp[:, n], xh[:, n]).then_inc(xp_in[n], 16)
            sync.dma_start(c_sb[:], cin).then_inc(c_in, 16)
            sync.dma_start(wmod_sb[:], wmod).then_inc(c_in, 16)
            sync.dma_start(con[:], consts).then_inc(con_in, 16)
            sync.dma_start(encq_sb[:], encq).then_inc(wq_in, 16)
            for dst, src in ((encv_sb, encv), (w1_sb, w1), (b1_sb, b1), (w2_sb, w2), (b2_sb, b2), (base_sb, base),
                             (hebu_sb, hebu), (hebv_sb, hebv), (dec_sb, dec), (wr_sb, wr), (a_sb, amat), (b_sb, bmat)):
                sync.dma_start(dst[:], src).then_inc(wts_in, 16)
            sync.dma_start(x0_sb[:], x.rearrange("(b t) d -> b t d", b=NB)[:, 0, :]).then_inc(wts_in, 16)
            for n in range(2, 4):
                sync.dma_start(xp[:, n], xh[:, n]).then_inc(xp_in[n], 16)
            with sync.Fori(4, 2 * NB - 3, 4) as n0:
                for u in range(4):
                    sync.wait_ge(xn_ready, n0 - 3 + u)
                    sync.dma_start(xp[:, u], xh[:, bass.ds(n0 + u, 1)].squeeze(1)).then_inc(xp_in[u], 16)

            xc = x.rearrange("(n p) d -> p n d", p=P)
            oc = out.rearrange("(n p) d -> p n d", p=P)

            def step(i, ph):
                k = i - 3
                if there(i, -3):
                    s = (ph - 3) % 2
                    sync.wait_ge(yo_ready, k + 1)
                    sync.dma_start(oc[:, bass.ds(k, 1)].squeeze(1), yo[:, s]).then_inc(out_in[s], 16)
                k, s = i + 3, (ph + 3) % 2
                if there(i, 3):
                    sync.wait_ge(nst_ready, k + 1)
                    for g in range(NG):
                        n_g = nst[g:NH:NG, s]
                        sync.dma_start(sst[HD:P:32, s, g, :], n_g).then_inc(rows_in[s], 16)
                        sync.dma_start(tst[HD + 1:P:32, s, g, :], nst[g:NH:NG, s, WIN:3 * WIN]).then_inc(rows_in[s], 16)
                k = i + 1
                if there(i, 1):
                    need(sync, att_ready, k - 3)
                    sync.dma_start(xs[:, (ph + 1) % 4], xc[:, bass.ds(k, 1)].squeeze(1)).then_inc(xs_in[(ph + 1) % 4], 16)
            steps(sync, step)
            for s in range(2):
                sync.wait_ge(out_in[s], 16 * NCH // 2)

        @block.gpsimd
        def _(pool):
            links = [0]

            def link(ins):
                links[0] += 1
                ins.then_inc(pool_chain, 1)
                pool.wait_ge(pool_chain, links[0])

            for col, value in enumerate((EPS_LN, 1e-8, 1.0, 0.0)):
                nc.gpsimd.memset(bias[:, col:col + 1], value).then_inc(bias_set, 1)
            nc.gpsimd.memset(udiag[:], 0.0).then_inc(ones_set, 1)
            for s in range(4):
                nc.gpsimd.memset(vst[:, s, :, :, HD:VD], 1.0).then_inc(ones_set, 1)
            pool.wait_ge(con_in, 16)
            nc.gpsimd.tensor_copy(ident_bf[:], ident).then_inc(bf_set, 1)
            nc.gpsimd.tensor_copy(mask_bf[:], con[:, C_MASK:C_MASK + 4 * WIN]).then_inc(bf_set, 1)
            pool.wait_ge(wts_in, 16 * 13)
            pool.wait_ge(ones_set, 1)
            hk = NH * RANK
            for g in range(NG):
                blk = con[0:hk, C_BLK + g * NR:C_BLK + (g + 1) * NR].unsqueeze(2).broadcast_to([hk, NR, HD])
                for dst, src in ((udiag[:, g, :, 0:HD], hebu_sb), (vdiag[:, g], hebv_sb)):
                    nc.gpsimd.tensor_tensor(dst, src[:].unsqueeze(1).broadcast_to([hk, NR, HD]), blk,
                                            ALU.mult).then_inc(diag_ready, 1)
            with pool.Fori(0, NB) as b:
                c0 = b * TP
                pool.wait_ge(hT_ready, 2 * b + 1)
                nc.gpsimd.tensor_copy(hT_all[:, bass.ds(c0, WIN)],
                                      hT_all[:, bass.ds(c0 + WIN, 1)].broadcast_to([P, WIN])).then_inc(pads_ready, 1)
                pool.wait_ge(q_ready, 4 * b + 2)
                nc.gpsimd.tensor_copy(qT_all[:, :, bass.ds(c0, WIN)],
                                      qT_all[:, :, bass.ds(c0 + WIN, 1)].broadcast_to([P, NG, WIN])).then_inc(pads_ready, 1)

            pool.wait_ge(aS_ready, 1)
            pool.wait_ge(pads_ready, 2 * NB)
            pool.wait_ge(q_ready, 4 * NB)

            def step(i, ph):
                k, s, s4 = i - 1, (ph - 1) % 2, (ph - 1) % 4
                if there(i, -1):
                    pool.wait_ge(wsel_ready, k + 1)
                    need(pool, wt_ready, 8 * (k - 1))
                    nc.gpsimd.tensor_tensor(
                        wun[:, s].rearrange("p h (v j) -> p h v j", v=2),
                        work[:, s].rearrange("p (h j) -> p h j", h=NH).unsqueeze(2).broadcast_to([P, NH, 2, WIN]),
                        unf.unsqueeze(1).broadcast_to([P, NH, 2, WIN]), ALU.mult).then_inc(w_ready, 1)
                k, s, s4 = i - 2, ph % 2, (ph - 2) % 4
                if there(i, -2):
                    pool.wait_ge(rnn_ready, k + 1)
                    nc.gpsimd.tensor_tensor(hsc[:], gat[:, s], rnn[:, s], ALU.mult).then_inc(mix_step, 1)
                    pool.wait_ge(rden_ready, k + 1)
                    h3 = "p (h e) -> p h e"
                    nc.gpsimd.tensor_tensor(t1[:].rearrange(h3, h=NH), cst[:, s, :, 0:HD],
                                            rden[:, s].unsqueeze(2).broadcast_to([P, NH, HD]), ALU.mult).then_inc(mix_step, 1)
                    pool.wait_ge(mix_step, 4 * k + 1)
                    nc.gpsimd.tensor_tensor(t2[:].rearrange(h3, h=NH), qh[:, s4, 1].rearrange(h3, h=NH),
                                            hsc[:].unsqueeze(2).broadcast_to([P, NH, HD]), ALU.mult).then_inc(mix_step, 1)
                    pool.wait_ge(mix_step, 4 * k + 3)
                    nc.gpsimd.tensor_tensor(t1[:], t1[:], t2[:], ALU.add).then_inc(mix_step, 1)
                    pool.wait_ge(mix_step, 4 * k + 4)
                    need(pool, po_ready, k - 1)
                    nc.gpsimd.tensor_tensor(osp[:, s], t1[:], qh[:, s4, 0], ALU.mult).then_inc(osp_ready, 1)
                k, s = i - 1, (ph - 1) % 2
                if there(i, -1):
                    wait_alone(pool, n2_ready, k + 1)
                    nc.gpsimd.tensor_scalar(gat[:, s], n2[:, s], GATE2, 0.1, ALU.is_gt, ALU.mult).then_inc(n2g_ready, 1)
                    nc.gpsimd.tensor_scalar(n2g[:, s], n2[:, s], 1e-18, None, ALU.max).then_inc(n2g_ready, 1)
                k, s = i + 3, (ph + 3) % 2
                if there(i, 3):
                    b, c0 = k // CPB, column(k)
                    wait_alone(pool, dist_ready, k - 1)
                    win = qT_all[:, :, bass.ds(c0, 3 * WIN)]
                    nc.gpsimd.tensor_tensor(sst[:, s], win, aS[:, :, bass.ds(b, 1)].broadcast_to([P, NG, 3 * WIN]),
                                            ALU.mult).then_inc(s_ready, 1)
                    nc.gpsimd.tensor_copy(tst[:, s], qT_all[:, :, bass.ds(c0 + WIN, CH)]).then_inc(opnd_ready, 1)
                    nc.gpsimd.tensor_copy(hst[:, s], hT_all[:, bass.ds(c0, 3 * WIN)]).then_inc(opnd_ready, 1)
                    pool.wait_ge(s_ready, k + 1)
                    wait_alone(pool, pn_ready, k - 1)
                    nc.gpsimd.tensor_tensor(sqs[:, s], sst[:, s], win, ALU.mult).then_inc(opnd_ready, 1)
                k, s4 = i, ph % 4
                if there(i, 0):
                    pool.wait_ge(qhs_ready, k + 1)
                    need(pool, n2_ready, k)
                    nc.gpsimd.tensor_tensor(qsq[:], qh[:, s4, 0], qh[:, s4, 0], ALU.mult).then_inc(qsq_ready, 1)

            def routing(i):
                if i == 1:
                    pool.wait_ge(gb_ready, 2)

            steps(pool, step, routing)

        @block.scalar
        def _(act):
            act.preload_act_table_set("natural_log_exp_and_others")
            act.wait_ge(c_in, 32)
            nc.scalar.activation(ec[:], c_sb[:], ACT.Exp, scale=-1.0).then_inc(ec_ready, 1)
            act.wait_ge(pmod_ready, 1)
            nc.scalar.activation(modT[:].rearrange("p j b -> p (j b)"), psC[:, 0:6 * NB], ACT.Copy).then_inc(modT_ready, 1)
            act.wait_ge(pmod_ready, 2)
            for j in range(2):
                nc.scalar.activation(modn[:, j * 384:(j + 1) * 384], psW[0:NB, j, 0:384], ACT.Copy).then_inc(modn_ready, 1)
            act.wait_ge(bias_set, 4)
            act.wait_ge(modT_ready, 2)
            act.wait_ge(con_in, 16)
            def invstd(n, u):
                act.wait_ge(mv_ready, 4 * n + 4)
                nc.scalar.activation(rs_p[:, u], mv_p[:, u, :, 1], ACT.Ln, bias=bias[:, 0:1]).then_inc(lnv_p, 1)
                act.wait_ge(lnv_p, n + 1)
                nc.scalar.activation(rs_p[:, u], rs_p[:, u], ACT.Exp, scale=-0.5).then_inc(rs_ready, 1)

            def columns(n):
                return bass.ds((n // 2) * TP + WIN + (n % 2) * HALF, HALF)

            def to_hT(n, u):
                b = n // 2
                act.wait_ge(pT_ready, n + 1)
                nc.scalar.activation(hT_all[:, columns(n)], psW[:, u % 2], ACT.Identity, bias=modT[:, 0, bass.ds(b, 1)],
                                     scale=modT[:, 1, bass.ds(b, 1)]).then_inc(hT_ready, 1)

            def to_q(n, u):
                for g in range(NG):
                    act.wait_ge(pq_ready, 2 * n + g + 1)
                    nc.scalar.activation(qT_all[:, g, columns(n)], psD[:, 2 * (u % 2) + g], ACT.Relu,
                                         bias=con[:, C_ROW + 2:C_ROW + 3],
                                         accum_out=qsum[:, g, u % 2, bass.ds(n // 2, 1)]).then_inc(q_ready, 1)

            invstd(0, 0)
            invstd(1, 1)
            to_hT(0, 0)
            with act.Fori(0, 2 * NB - 7, 4) as n0:
                for u in range(4):
                    invstd(n0 + u + 2, (u + 2) % 4)
                    to_hT(n0 + u + 1, (u + 1) % 4)
                    to_q(n0 + u, u)
            for n in range(2 * NB - 4, 2 * NB):
                if n + 2 < 2 * NB:
                    invstd(n + 2, (n + 2) % 4)
                if n + 1 < 2 * NB:
                    to_hT(n + 1, (n + 1) % 4)
                to_q(n, n % 4)
            act.wait_ge(pheb_ready, 2)
            for g in range(NG):
                nc.scalar.activation(selheb[:, g, 1], psX[:, 256 + g * 64:320 + g * 64], ACT.Copy).then_inc(selheb_ready, 1)
            act.wait_ge(pm1_ready, 1)
            nc.scalar.activation(h1[:], psX[0:64, 0:NB], ACT.Gelu, bias=b1_sb[:]).then_inc(h1_ready, 1)
            act.preload_act_table_set("natural_log_exp_and_others")
            act.wait_ge(p0_ready, 1)
            nc.scalar.activation(z8[:, 0:2].rearrange("p a b -> p (a b)"), psW[0:NB, 1, 0:256], ACT.Copy).then_inc(r0_act, 1)
            nc.scalar.activation(z8[:, 2], psW[0:NB, 1, 256:384], ACT.Relu).then_inc(r0_act, 1)
            act.wait_ge(r0_dve, 1)
            nc.scalar.activation(s8[:, 2], s8[:, 1], ACT.Ln).then_inc(r0_act, 1)
            act.wait_ge(r0_act, 3)
            nc.scalar.activation(s8[:, 3], s8[:, 2], ACT.Exp, scale=-0.5).then_inc(r0_act, 1)
            act.wait_ge(z_ready, 1)
            nc.scalar.activation(sp[:, 1], sp[:, 0], ACT.Abs).then_inc(sp_act, 1)
            act.wait_ge(sp_act, 1)
            nc.scalar.activation(sp[:, 2], sp[:, 1], ACT.Exp, scale=-1.0).then_inc(sp_act, 1)
            act.wait_ge(sp_dve, 1)
            nc.scalar.activation(sp[:, 4], sp[:, 3], ACT.Ln).then_inc(sp_act, 1)

            def routing(i):
                if i == -3:
                    act.wait_ge(r0_dve, 4)
                    nc.scalar.activation(s8[:, 7, 0:1], s8[:, 6, 1:2], ACT.Ln, bias=bias[0:NB, 0:1]).then_inc(r0_act, 1)
                    act.wait_ge(r0_act, 5)
                    nc.scalar.activation(s8[:, 7, 1:2], s8[:, 7, 0:1], ACT.Exp, scale=-0.5).then_inc(r0_act, 1)
                if i == -2:
                    act.wait_ge(r0_dve, 7)
                    nc.scalar.activation(s8[:, 11], s8[:, 8], ACT.Exp, bias=s8[:, 10, 0:1]).then_inc(r0_act, 1)

            def step(i, ph):
                k, s, s4 = i - 1, (ph - 1) % 2, (ph - 1) % 4
                if there(i, -1):
                    act.wait_ge(picked, 16 * (k + 1))
                    nc.scalar.activation(work[:, s], work[:, s], ACT.Square).then_inc(square_done, 1)
                    act.wait_ge(square_done, k + 1)
                    nc.scalar.activation(work[:, s], work[:, s], ACT.Exp, scale=-1.0).then_inc(wsel_ready, 1)
                k, s, s4 = i + 1, (ph + 1) % 2, (ph + 1) % 4
                if there(i, 1):
                    act.wait_ge(dist_ready, k + 1)
                    need(act, picked, 16 * (k - 2) + 4)
                    nc.scalar.activation(key[:, s].rearrange("p (r x) -> p r x", r=NR), dA, ACT.Relu).then_inc(amin_ready, 1)
                    need(act, c_ready, k - 3)
                    nc.scalar.activation(vst[:, s4, :, :, 0:HD], pV.rearrange("p (v h e) -> p h v e", v=2, h=NH),
                                         ACT.Relu).then_inc(vst_ready, 1)
                    need(act, osp_ready, k - 3)
                    nc.scalar.activation(qh[:, s4].rearrange("p a c -> p (a c)"), pQH, ACT.Copy).then_inc(qhs_ready, 1)
                k, s = i - 3, (ph - 3) % 2
                if there(i, -3):
                    b = k // CPB
                    act.wait_ge(pn2_ready, k + 1)
                    need(act, y_ready, k - 1)
                    nc.scalar.activation(h2T[:, s], pN2, ACT.Identity, bias=modT[:, 3, bass.ds(b, 1)],
                                         scale=modT[:, 4, bass.ds(b, 1)]).then_inc(h2T_ready, 1)
                k, s = i - 1, (ph - 1) % 2
                if there(i, -1):
                    for w in range(2):
                        act.wait_ge(wt_ready, 8 * k + 4 * w + 4)
                        need(act, c_ready, k - 1)
                        nc.scalar.activation(wts[:, s, 4 * w:4 * w + 4].rearrange("p h t -> p (h t)"), psW[:, w],
                                             ACT.Copy).then_inc(wts_ready, 1)
                k, s = i - 3, (ph - 3) % 2
                if there(i, -3):
                    act.wait_ge(y_ready, k + 1)
                    need(act, out_in[s], 16 * (k // 2))
                    nc.scalar.activation(yo[:, s], pY, ACT.Copy).then_inc(yo_ready, 1)
                k, s = i - 2, ph % 2
                if there(i, -2):
                    act.wait_ge(po_ready, k + 1)
                    nc.scalar.activation(oT[:, s], pO, ACT.Copy).then_inc(oT_ready, 1)
                    act.wait_ge(att_ready, k + 1)
                    nc.scalar.activation(x2[:, s], pAtt, ACT.Copy).then_inc(x2_ready, 1)
                k, s = i + 1, (ph + 1) % 2
                if there(i, 1):
                    act.wait_ge(d2_ready, k + 1)
                    nc.scalar.activation(key[:, s], key[:, s], ACT.Ln, bias=bias[:, 1:2]).then_inc(ln_done, 1)
                    act.wait_ge(ln_done, k + 1)
                    nc.scalar.activation(key[:, s], key[:, s], ACT.Exp, scale=0.25).then_inc(key_ready, 1)
                k, s = i - 1, (ph - 1) % 2
                if there(i, -1):
                    act.wait_ge(c_ready, k + 1)
                    need(act, osp_ready, k - 1)
                    pc = pC.rearrange("p (h v e) -> p h v e", h=NH, v=2)
                    nc.scalar.activation(cst[0:WIN, s], pc[0:WIN, :, 0], ACT.Copy).then_inc(cst_ready, 1)
                    nc.scalar.activation(cst[WIN:P, s], pc[WIN:P, :, 1], ACT.Copy).then_inc(cst_ready, 1)
                    act.wait_ge(n2g_ready, 2 * (k + 1))
                    nc.scalar.activation(lnn[:], n2g[:, s], ACT.Ln).then_inc(lnn_done, 1)
                    act.wait_ge(lnn_done, k + 1)
                    nc.scalar.activation(rnn[:, s], lnn[:], ACT.Exp, scale=-0.5).then_inc(rnn_ready, 1)
                k, s = i + 3, (ph + 3) % 2
                if there(i, 3):
                    act.wait_ge(pn_ready, k + 1)
                    need(act, rows_in[s], 64 * (k // 2))
                    nc.scalar.activation(nst[:, s], pN, ACT.Copy).then_inc(nst_ready, 1)
                k, s = i - 2, ph % 2
                if there(i, -2):
                    act.wait_ge(mvc_ready, k + 1)
                    nc.scalar.activation(lv_c[:], mv_c[:, s, 1:2], ACT.Ln, bias=bias[:, 0:1]).then_inc(lnc_done, 1)
                    act.wait_ge(lnc_done, k + 1)
                    nc.scalar.activation(rs_c[:, s:s + 1], lv_c[:], ACT.Exp, scale=-0.5).then_inc(rsc_ready, 1)

            steps(act, step, routing)

        @block.vector
        def _(dve):
            links = [0]

            def link(ins):
                links[0] += 1
                ins.then_inc(dve_chain, 1)
                dve.wait_ge(dve_chain, links[0])

            v = nc.vector
            dve.wait_ge(ec_ready, 1)
            link(v.tensor_scalar(ec[:], ec[:], 1.0, None, ALU.add))
            link(v.reciprocal(ec[:], ec[:]))
            v.tensor_tensor(sil[:], c_sb[:], ec[:], ALU.mult).then_inc(sil_ready, 1)
            dve.wait_ge(modT_ready, 1)
            for j in (1, 4):
                last = v.tensor_scalar(modT[:, j], modT[:, j], 1.0, None, ALU.add)
            last.then_inc(modT_ready, 1)
            dve.wait_ge(modn_ready, 2)
            gview = modn[:].rearrange("b (u v d) -> b u v d", u=2, v=3)[:, :, 2]
            link(v.tensor_scalar(gsgn[:], gview, 0.0, 2.0, ALU.is_ge, ALU.mult))
            link(v.tensor_scalar(gabs[:], gview, -1.0, None, ALU.mult))
            link(v.tensor_tensor(gabs[:], gabs[:], gview, ALU.max))
            link(v.tensor_scalar(gabs[:], gabs[:], 0.25, None, ALU.max))
            v.scalar_tensor_tensor(out=gn[:], in0=gsgn[:], scalar=-1.0, in1=gabs[:], op0=ALU.add,
                                   op1=ALU.mult).then_inc(gates_n_ready, 1)
            dve.wait_ge(con_in, 16)
            for g in range(NG):
                v.tensor_copy(selheb[:, g, 0], con[:, C_SELQ:C_SELQ + NR * HD]).then_inc(selheb_ready, 1)

            def stats(n, u):
                dve.wait_ge(xp_in[u], 16 * (n // 4) + 16)
                for c in range(4):
                    v.bn_stats(st_p[:, u, c], xp[:, u, c]).then_inc(st_ready, 1)
                for c in range(4):
                    wait_alone(dve, st_ready, 4 * n + c + 1)
                    v.bn_aggr(mv_p[:, u, c], st_p[:, u, c]).then_inc(mv_ready, 1)

            def normalise(n, u):
                dve.wait_ge(rs_ready, n + 1)
                need(dve, pT_ready, n - 1)
                for c in range(4):
                    last = v.tensor_scalar(xn[:, u % 2, c], xp[:, u, c], mv_p[:, u, c, 0:1],
                                           rs_p[:, u, c:c + 1], ALU.subtract, ALU.mult)
                last.then_inc(xn_ready, 1)

            def every_8th(b):
                dve.wait_ge(q_ready, 4 * b + 4)
                v.tensor_reduce(qsum8[:, :, bass.ds(b, 1)], qT_all[:, :, bass.ds(b * TP + WIN, T // 8, step=8)],
                                AX_X, ALU.add).then_inc(qsum8_ready, 1)

            stats(0, 0)
            stats(1, 1)
            normalise(0, 0)
            stats(2, 2)
            normalise(1, 1)
            with dve.Fori(2, 2 * NB - 5, 4) as n0:
                for u in range(4):
                    n = n0 + u
                    stats(n + 1, (u + 3) % 4)
                    normalise(n, (u + 2) % 4)
                    if u % 2 == 1:
                        every_8th((n0 + u - 3) // 2)
            stats(2 * NB - 1, 3)
            normalise(2 * NB - 2, 2)
            normalise(2 * NB - 1, 3)
            every_8th(NB - 2)
            every_8th(NB - 1)
            link(v.tensor_tensor(sig[:], qsum[:, :, 0], qsum[:, :, 1], ALU.add))
            link(v.tensor_scalar(sig[:], sig[:], 1.0 / T, None, ALU.mult))
            dve.wait_ge(qsum8_ready, NB)
            v.scalar_tensor_tensor(out=sig[:], in0=qsum8[:], scalar=0.5 * 8 / T, in1=sig[:], op0=ALU.mult,
                                   op1=ALU.add).then_inc(sig_ready, 1)
            def gate_weights(pr):
                dve.wait_ge(pgate_ready, pr + 1)
                two = slice(2 * pr, 2 * pr + 2)
                gate_ps = psC[:].rearrange("p (b u d) -> p b u d", b=2, u=2)
                v.tensor_tensor(dec_b[:, two], dec_sb[:].unsqueeze(1).broadcast_to([P, 2, D]), gate_ps[:, :, 0], ALU.mult)
                v.tensor_copy(g_b[:, two], gate_ps[:, :, 1]).then_inc(gatew_ready, 1)

            dve.wait_ge(wts_in, 16 * 13)
            gate_weights(0)
            q0, hb0, v0 = z8[:, 0], z8[:, 1], z8[:, 2]
            h3 = "p (h e) -> p h e"
            dve.wait_ge(r0_act, 2)
            link(v.tensor_tensor(z8[:, 3], q0, q0, ALU.mult))
            link(v.tensor_reduce(s8[:, 0], z8[:, 3].rearrange(h3, h=NH), AX_X, ALU.add))
            v.tensor_scalar(s8[:, 1], s8[:, 0], 1e-18, None, ALU.max).then_inc(r0_dve, 1)
            link(v.tensor_scalar(s8[:, 4], s8[:, 0], GATE2, 0.1, ALU.is_gt, ALU.mult))
            gate_weights(1)
            dve.wait_ge(pm2_ready, 1)
            z = sp[:, 0].rearrange("p (g b) -> p g b", g=NG)
            for g in range(NG):
                link(v.tensor_scalar(z[:, g], psX[:, 64 + g * NB:64 + (g + 1) * NB], b2_sb[:, g:g + 1], 0.1, ALU.add, ALU.mult))
            for g in range(NG):
                last = v.tensor_scalar(z[:, g], z[:, g], base_sb[:, g:g + 1], None, ALU.add)
            last.then_inc(z_ready, 1)
            dve.wait_ge(r0_act, 4)
            link(v.tensor_tensor(s8[:, 5], s8[:, 4], s8[:, 3], ALU.mult))
            link(v.tensor_tensor(z8[:, 4].rearrange(h3, h=NH), hb0.rearrange(h3, h=NH),
                                 s8[:, 5].unsqueeze(2).broadcast_to([NB, NH, HD]), ALU.mult))
            total = TOPK * float(np.exp(-np.sqrt(1e-8)))
            link(v.scalar_tensor_tensor(out=z8[:, 5], in0=v0, scalar=total / (total + 1e-8), in1=z8[:, 4],
                                        op0=ALU.mult, op1=ALU.add))
            v.tensor_tensor(z8[:, 6], z8[:, 5], q0, ALU.mult).then_inc(r0_dve, 1)
            dve.wait_ge(sp_act, 2)
            v.tensor_scalar(sp[:, 3], sp[:, 2], 1.0, None, ALU.add).then_inc(sp_dve, 1)
            dve.wait_ge(sp_dve, 1)
            link(v.tensor_scalar(sp[:, 5], sp[:, 3], -1.0, None, ALU.add))
            link(v.tensor_scalar(sp[:, 6], sp[:, 5], 0.0, None, ALU.is_equal))
            link(v.tensor_tensor(sp[:, 5], sp[:, 5], sp[:, 6], ALU.add))
            link(v.reciprocal(sp[:, 5], sp[:, 5]))
            dve.wait_ge(sp_act, 3)
            link(v.tensor_tensor(sp[:, 6], sp[:, 6], sp[:, 4], ALU.add))
            link(v.tensor_tensor(sp[:, 6], sp[:, 6], sp[:, 5], ALU.mult))
            link(v.tensor_tensor(sp[:, 6], sp[:, 6], sp[:, 2], ALU.mult))
            link(v.scalar_tensor_tensor(out=sp[:, 7], in0=sp[:, 0], scalar=0.0, in1=sp[:, 6], op0=ALU.max, op1=ALU.add))
            v.tensor_scalar(aS[:].rearrange("p g b -> p (g b)"), sp[:, 7], con[:, C_ROW:C_ROW + 1],
                            con[:, C_ROW + 1:C_ROW + 2], ALU.mult, ALU.add).then_inc(aS_ready, 1)
            dve.wait_ge(r0_pe, 1)
            v.tensor_copy(o0T[:], psX[:, 128:128 + NB]).then_inc(r0_dve, 1)
            gate_weights(2)
            dve.wait_ge(r0_pe, 2)
            link(v.tensor_tensor(z8[:, 7], psX[0:NB, 256:384], gn[:, 0], ALU.mult))
            link(v.tensor_tensor(z8[:, 7], z8[:, 7], x0_sb[:], ALU.add))
            link(v.bn_stats(s8[:, 9, 0:6], z8[:, 7]))
            v.bn_aggr(s8[:, 6, 0:2], s8[:, 9, 0:6]).then_inc(r0_dve, 1)
            gate_weights(3)
            dve.wait_ge(r0_act, 6)
            v.tensor_scalar(z8[:, 8], z8[:, 7], s8[:, 6, 0:1], s8[:, 7, 1:2], ALU.subtract, ALU.mult).then_inc(r0_dve, 1)
            dve.wait_ge(r0_pe, 3)
            link(v.tensor_tensor(h0T[:], psX[:, 136:136 + NB], modT[:, 4], ALU.mult))
            v.tensor_tensor(h0T[:], h0T[:], modT[:, 3], ALU.add).then_inc(r0_dve, 1)

            def routing(i):
                if i == -1:
                    dve.wait_ge(r0_pe, 4)
                    lg = s8[:, 8]
                    link(v.tensor_copy(lg, psX[0:NB, 144:144 + NE]))
                    link(v.max(s8[:, 9], lg))
                    v.tensor_scalar(s8[:, 10, 0:1], s8[:, 9, 0:1], -1.0, None, ALU.mult).then_inc(r0_dve, 1)
                    link(v.tensor_scalar(s8[:, 12], lg, s8[:, 9, 1:2], None, ALU.is_gt))
                    link(v.tensor_scalar(s8[:, 13], lg, s8[:, 9, 1:2], None, ALU.is_equal))
                    link(v.tensor_copy(s8[:, 14], s8[:, 13]))
                    for sh in (1, 2, 4):
                        link(v.tensor_copy(s8[:, 15], s8[:, 14]))
                        link(v.tensor_tensor(s8[:, 14, sh:NE], s8[:, 14, sh:NE], s8[:, 15, 0:NE - sh], ALU.add))
                    link(v.tensor_reduce(s8[:, 16, 0:1], s8[:, 12], AX_X, ALU.add))
                    link(v.tensor_scalar(s8[:, 16, 1:2], s8[:, 16, 0:1], -1.0, 2.0, ALU.mult, ALU.add))
                    link(v.tensor_scalar(s8[:, 17], s8[:, 14], s8[:, 16, 1:2], None, ALU.is_le))
                    link(v.tensor_tensor(s8[:, 17], s8[:, 17], s8[:, 13], ALU.mult))
                    link(v.tensor_tensor(s8[:, 17], s8[:, 17], s8[:, 12], ALU.add))
                    dve.wait_ge(r0_act, 7)
                    link(v.tensor_tensor(s8[:, 18], s8[:, 11], s8[:, 17], ALU.mult))
                    link(v.tensor_reduce(s8[:, 19, 0:1], s8[:, 18], AX_X, ALU.add))
                    link(v.reciprocal(s8[:, 19, 1:2], s8[:, 19, 0:1]))
                    v.tensor_scalar(s8[:, 20], s8[:, 18], s8[:, 19, 1:2], None, ALU.mult).then_inc(r0_dve, 1)
                    dve.wait_ge(r0_pe, 5)
                    v.tensor_copy(gateT[:], psX[0:NE, 152:152 + NB]).then_inc(r0_dve, 1)
                    dve.wait_ge(r0_pe, 6)
                    link(v.tensor_copy(gate_er[:].rearrange("p k b -> p (k b)"), psX[:, 160:160 + 4 * NB]))
                if i == 0:
                    for kt in range(4):
                        v.tensor_tensor(bsc[:, kt], b_sb[:, kt].unsqueeze(1).broadcast_to([P, NB, D]),
                                        gate_er[:, kt].unsqueeze(2).broadcast_to([P, NB, D]), ALU.mult).then_inc(bsc_ready, 1)
                if i == 1:
                    for half, bank in enumerate((psC, psX)):
                        four = slice(4 * half, 4 * half + 4)
                        dve.wait_ge(pG_ready, half + 1)
                        link(v.tensor_tensor(mI[:], bank[:].rearrange("p (b d) -> p b d", b=4),
                                             ident.unsqueeze(1).broadcast_to([P, 4, D]), ALU.add))
                        v.tensor_tensor(g_b[:, four], g_b[:, four], mI[:], ALU.mult).then_inc(gb_ready, 1)
                        if half == 0:
                            dve.wait_ge(gb_ready, 1)

            def rounds(i, ph, rnd):
                s = ph % 2
                src = key[:, s] if rnd == 0 else work[:, s]
                for half in range(2):
                    wait_alone(dve, picked, 16 * i + 4 * (rnd - 1) + 3 + half)
                    for h in range(4 * half, 4 * half + 4):
                        last = v.max(m8[:, h], src[:, h * WIN:(h + 1) * WIN])
                    last.then_inc(picked, 1)
                for half in range(2):
                    wait_alone(dve, picked, 16 * i + 4 * rnd + 1 + half)
                    for h in range(4 * half, 4 * half + 4):
                        cols = slice(h * WIN, (h + 1) * WIN)
                        last = v.match_replace(work[:, s, cols], m8[:, h], src[:, cols], GONE)
                    last.then_inc(picked, 1)

            def step(i, ph):
                if there(i, 0):
                    dve.wait_ge(key_ready, i + 1)
                    wait_alone(dve, w_ready, i - 1)
                    rounds(i, ph, 0)
                k, s = i - 3, (ph - 3) % 2
                if there(i, -3):
                    dve.wait_ge(rsc_ready, k + 1)
                    need(dve, pn2_ready, k - 1)
                    v.tensor_scalar(n_c[:, s], x2[:, s], mv_c[:, s, 0:1], rs_c[:, s:s + 1], ALU.subtract,
                                    ALU.mult).then_inc(nc_ready, 1)
                k, s = i - 1, (ph - 1) % 2
                if there(i, -1):
                    dve.wait_ge(qsq_ready, k + 1)
                    need(dve, n2g_ready, 2 * (k - 1))
                    v.tensor_reduce(n2[:, s], qsq[:].rearrange("p (h e) -> p h e", h=NH), AX_X, ALU.add).then_inc(n2_ready, 1)
                if there(i, 0):
                    rounds(i, ph, 1)
                k, s = i + 1, (ph + 1) % 2
                if there(i, 1):
                    dve.wait_ge(qhs_ready, k + 1)
                    e = key[:, s].rearrange("p (r x) -> p r x", r=NR)
                    v.scalar_tensor_tensor(out=e, in0=dB, scalar=0.0, in1=e, op0=ALU.max, op1=ALU.min).then_inc(d2_ready, 1)
                if there(i, 0):
                    rounds(i, ph, 2)
                k, s = i - 2, ph % 2
                if there(i, -2):
                    dve.wait_ge(x2_ready, k + 1)
                    v.bn_stats(st_c[:], x2[:, s]).then_inc(stc_ready, 1)
                    wait_alone(dve, stc_ready, k + 1)
                    v.bn_aggr(mv_c[:, s], st_c[:]).then_inc(mvc_ready, 1)
                if there(i, 0):
                    rounds(i, ph, 3)
                k, s = i - 1, (ph - 1) % 2
                if there(i, -1):
                    dve.wait_ge(cst_ready, 2 * (k + 1))
                    need(dve, rden_ready, k - 1)
                    v.tensor_scalar(den[:, s], cst[:, s, :, HD], 1e-8, None, ALU.add).then_inc(den_done, 1)
                    dve.wait_ge(den_done, k + 1)
                    v.reciprocal(rden[:, s], den[:, s]).then_inc(rden_ready, 1)

            steps(dve, step, routing)

        @block.tensor
        def _(pe):
            mm = nc.tensor.matmul
            pe.wait_ge(sil_ready, 1)
            for j in range(6):
                last = mm(psC[:, j * NB:(j + 1) * NB], wmod_sb[:, j * D:(j + 1) * D], sil[:], start=True, stop=True)
            last.then_inc(pmod_ready, 1)
            for j in range(2):
                last = mm(psW[0:NB, j, 0:384], sil[:], wmod_sb[:, j * 384:(j + 1) * 384], start=True, stop=True)
            last.then_inc(pmod_ready, 1)
            pe.wait_ge(con_in, 16)
            pe.wait_ge(diag_ready, 2 * NG)
            for g in range(NG):
                mm(psX[:, 256 + g * 64:320 + g * 64], udiag[:, g].rearrange("k r e -> k (r e)"),
                   vdiag[:, g].rearrange("k r e -> k (r e)"), start=True, stop=True).then_inc(pheb_ready, 1)
            pe.wait_ge(wq_in, 16)
            pe.wait_ge(modn_ready, 2)
            def to_pT(n, u):
                pe.wait_ge(xn_ready, n + 1)
                need(pe, hT_ready, n - 1)
                for c in range(4):
                    last = nc.tensor.transpose(psW[:, u % 2, c * P:(c + 1) * P], xn[:, u % 2, c], ident)
                last.then_inc(pT_ready, 1)

            def to_pq(n, u):
                pe.wait_ge(hT_ready, n + 1)
                for g in range(NG):
                    mm(psD[:, 2 * (u % 2) + g], encq_sb[:, g],
                       hT_all[:, bass.ds((n // 2) * TP + WIN + (n % 2) * HALF, HALF)],
                       start=True, stop=True).then_inc(pq_ready, 1)

            to_pT(0, 0)
            to_pT(1, 1)
            to_pq(0, 0)
            with pe.Fori(1, 2 * NB - 6, 4) as n0:
                for u in range(4):
                    to_pT(n0 + u + 1, u)
                    to_pq(n0 + u, u + 1)
            for n in range(2 * NB - 3, 2 * NB):
                if n + 1 < 2 * NB:
                    to_pT(n + 1, n + 1)
                to_pq(n, n)

            def gate_rows(pr):
                pe.wait_ge(gates_n_ready, 1)
                need(pe, gatew_ready, pr)
                for j in range(2):
                    last = mm(psC[:, j * 256:(j + 1) * 256], con[0:NB, 2 * pr + j:2 * pr + j + 1].broadcast_to([NB, P]),
                              gn[:].rearrange("b u d -> b (u d)"), start=True, stop=True)
                last.then_inc(pgate_ready, 1)

            gate_rows(0)
            pe.wait_ge(wts_in, 16 * 13)
            pe.wait_ge(sig_ready, 1)
            pe.wait_ge(selheb_ready, 2 * NG)
            for g in range(NG):
                last = mm(psX[0:64, 0:NB], w1_sb[:, g], sig[:, g], start=(g == 0), stop=(g == NG - 1))
            last.then_inc(pm1_ready, 1)
            pe.wait_ge(q_ready, 4 * NB)
            first = slice(WIN, NB * TP, TP)
            for g in range(NG):
                o = psW[0:NB, 1, 0:256].rearrange("p (a r g e) -> p a r g e", a=2, r=NR, g=NG)[:, :, :, g]
                mm(o, qT_all[:, g, first], selheb[:, g].rearrange("p a (r e) -> p a r e", r=NR), start=True, stop=True)
            mm(psW[0:NB, 1, 256:384], hT_all[:, first], encv_sb[:], start=True, stop=True).then_inc(p0_ready, 1)
            pe.wait_ge(h1_ready, 1)
            for g in range(NG):
                last = mm(psX[:, 64 + g * NB:64 + (g + 1) * NB], w2_sb[:, g], h1[:], start=True, stop=True)
            last.then_inc(pm2_ready, 1)
            gate_rows(1)
            pe.wait_ge(z_ready, 1)
            pe.wait_ge(r0_dve, 2)
            nc.tensor.transpose(psX[:, 128:128 + NB], z8[:, 6], con[0:NB, 0:NB]).then_inc(r0_pe, 1)
            gate_rows(2)
            pe.wait_ge(r0_dve, 3)
            mm(psX[0:NB, 256:384], o0T[:], dec_sb[:], start=True, stop=True).then_inc(r0_pe, 1)
            gate_rows(3)
            pe.wait_ge(r0_dve, 5)
            nc.tensor.transpose(psX[:, 136:136 + NB], z8[:, 8], con[0:NB, 0:NB]).then_inc(r0_pe, 1)
            pe.wait_ge(bf_set, 2)

            def routing(i):
                if i == -2:
                    pe.wait_ge(r0_dve, 6)
                    mm(psX[0:NB, 144:144 + NE], h0T[:], wr_sb[:], start=True, stop=True).then_inc(r0_pe, 1)
                    pe.wait_ge(r0_dve, 8)
                    nc.tensor.transpose(psX[0:NE, 152:152 + NB], s8[:, 20], con[0:NB, 0:NB]).then_inc(r0_pe, 1)
                    pe.wait_ge(r0_dve, 9)
                    for kt in range(4):
                        last = mm(psX[:, 160 + kt * NB:160 + (kt + 1) * NB], con[0:NE, C_EXP + kt * P:C_EXP + (kt + 1) * P],
                                  gateT[:], start=True, stop=True)
                    last.then_inc(r0_pe, 1)
                if i == 1:
                    pe.wait_ge(bsc_ready, 4)
                    pe.wait_ge(gatew_ready, NB // 2)
                    for half, bank in enumerate((psC, psX)):
                        for kt in range(4):
                            last = mm(bank[:], a_sb[:, kt], bsc[:, kt, 4 * half:4 * half + 4].rearrange("p b d -> p (b d)"),
                                      start=(kt == 0), stop=(kt == 3))
                        last.then_inc(pG_ready, 1)
                    pe.wait_ge(gb_ready, 2)

            def step(i, ph):
                k, s = i + 1, (ph + 1) % 2
                if there(i, 1):
                    pe.wait_ge(rows_in[s], 64 * (k // 2) + 64)
                    need(pe, d2_ready, k)
                    for r in range(NR):
                        mm(psD[:, r, 0:4 * WIN], ident_bf[:], mask_bf[:], start=True, stop=False, skip_group_check=True)
                    for g in range(NG):
                        for r in range(NR):
                            row = slice(32 * r, 32 * r + HD + 2)
                            ca, cb = g * WIN, 2 * WIN + g * WIN
                            mm(psD[:, r, ca:ca + WIN], tst[row, s, g], sst[row, s, g, WIN:2 * WIN],
                               start=False, stop=False, skip_group_check=True)
                            mm(psD[0:WIN, r, cb:cb + WIN], tst[row, s, g, 0:WIN], sst[row, s, g, 0:WIN],
                               start=False, stop=False, skip_group_check=True)
                            mm(psD[WIN:P, r, cb:cb + WIN], tst[row, s, g, WIN:CH], sst[row, s, g, 2 * WIN:3 * WIN],
                               start=False, stop=(g == NG - 1), skip_group_check=True)
                    mm(pV[:, P:2 * P], hst[:, s, WIN:3 * WIN], encv_sb[:], start=True, stop=True)
                    mm(pV[0:WIN, 0:P], hst[:, s, WIN:2 * WIN], encv_sb[:], start=True, stop=True)
                    mm(pV[WIN:P, 0:P], hst[:, s, 0:WIN], encv_sb[:], start=True, stop=True)
                    for g in range(NG):
                        o = pQH.rearrange("p (a r g e) -> p a r g e", a=2, r=NR, g=NG)[:, :, :, g]
                        last = mm(o, tst[:, s, g], selheb[:, g].rearrange("p a (r e) -> p a r e", r=NR),
                                  start=True, stop=True)
                    last.then_inc(dist_ready, 1)
                k, s = i - 3, (ph - 3) % 2
                if there(i, -3):
                    pe.wait_ge(nc_ready, k + 1)
                    need(pe, x2_ready, min(k + 1, NCH) if isinstance(k, int) else k + 1)
                    nc.tensor.transpose(pN2, n_c[:, s], ident).then_inc(pn2_ready, 1)
                k, s, s4 = i - 1, (ph - 1) % 2, (ph - 1) % 4
                if there(i, -1):
                    pe.wait_ge(w_ready, k + 1)
                    need(pe, nst_ready, min(k + 4, NCH) if isinstance(k, int) else k + 4)
                    for h in range(NH):
                        if h % 4 == 0:
                            need(pe, wts_ready, 2 * k - 1 + h // 4)
                        nc.tensor.transpose(psW[:, h // 4, (h % 4) * P:(h % 4 + 1) * P], wun[:, s, h],
                                            ident).then_inc(wt_ready, 1)
                k, s = i - 3, (ph - 3) % 2
                if there(i, -3):
                    pe.wait_ge(h2T_ready, k + 1)
                    mm(pY, ident, x2[:, s], start=True, stop=False)
                    mm(pY, h2T[:, s], g_b[:, bass.ds(k // CPB, 1)].squeeze(1), start=False, stop=True).then_inc(y_ready, 1)
                k, s, x4 = i - 2, ph % 2, (ph - 2) % 4
                if there(i, -2):
                    pe.wait_ge(osp_ready, k + 1)
                    need(pe, yo_ready, k)
                    nc.tensor.transpose(pO, osp[:, s], ident).then_inc(po_ready, 1)
                    pe.wait_ge(oT_ready, k + 1)
                    pe.wait_ge(xs_in[x4], 16 * (k // 4) + 16)
                    mm(pAtt, ident, xs[:, x4], start=True, stop=False)
                    mm(pAtt, oT[:, s], dec_b[:, bass.ds(k // CPB, 1)].squeeze(1), start=False, stop=True).then_inc(att_ready, 1)
                k, s, s4 = i - 1, (ph - 1) % 2, (ph - 1) % 4
                if there(i, -1):
                    need(pe, cst_ready, 2 * k)
                    pe.wait_ge(vst_ready, k + 1)
                    for h in range(NH):
                        if h % 4 == 0:
                            pe.wait_ge(wts_ready, 2 * k + 1 + h // 4)
                        last = mm(pC[:, h * 2 * VD:(h + 1) * 2 * VD], wts[:, s, h],
                                  vst[:, s4, h].rearrange("p v e -> p (v e)"), start=True, stop=True)
                    last.then_inc(c_ready, 1)
                k, s = i + 3, (ph + 3) % 2
                if there(i, 3):
                    pe.wait_ge(opnd_ready, 3 * (k + 1))
                    need(pe, nst_ready, k)
                    for g in range(NG):
                        last = mm(pN, seln[:, g], sqs[:, s, g], start=(g == 0), stop=(g == NG - 1))
                    last.then_inc(pn_ready, 1)

            steps(pe, step, routing)


def kernel(**inputs):
    import concourse.bacc as bacc
    from concourse.bass_utils import run_bass_kernel_spmd

    a = {k.replace("L0_", ""): np.asarray(v) for k, v in inputs.items()}

    def padded(w):
        w = w.reshape(w.shape[:-1] + (NR, NG, HD))
        w = np.moveaxis(w, -2, -3)
        w = np.pad(w, [(0, 0)] * (w.ndim - 1) + [(0, 32 - HD)])
        return w.reshape(w.shape[:-3] + (NG, P))

    encq = a["attn_enc_q"].transpose(1, 0, 2).reshape(D, P)
    arrays = {
        "x": a["attn_x"].reshape(NB * T, D),
        "encq": padded(encq),
        "encv": a["attn_enc_v"].transpose(1, 0, 2).reshape(D, P),
        "w1": padded(a["attn_metric_w1"].T).transpose(2, 1, 0),
        "b1": a["attn_metric_b1"].reshape(64, 1),
        "w2": padded(a["attn_metric_w2"]),
        "b2": padded(a["attn_metric_b2"]).T,
        "base": padded(a["attn_base_metric"].reshape(P)).T,
        "hebu": a["attn_hebb_U"].transpose(0, 2, 1).reshape(NH * RANK, HD),
        "hebv": a["attn_hebb_V"].reshape(NH * RANK, HD),
        "dec": a["attn_decoder"],
        "wr": a["ffn_Wr"].T,
        "amat": a["ffn_A"].reshape(4, P, D).transpose(1, 0, 2),
        "bmat": a["ffn_Bw"].transpose(0, 2, 1).reshape(4, P, D).transpose(1, 0, 2),
        "cin": a["c"].T,
        "wmod": a["wmod"],
        "consts": constants(),
    }
    nc = bacc.Bacc("TRN2", target_bir_lowering=False, num_devices=1)
    arrays = {f"in_{k}": np.ascontiguousarray(v) for k, v in arrays.items()}
    args = [nc.dram_tensor(k, v.shape, F32, kind="ExternalInput").ap() for k, v in arrays.items()]
    args.append(nc.dram_tensor("out_0", (NB * T, D), F32, kind="ExternalOutput").ap())
    adaln_block(nc, *args)
    r = run_bass_kernel_spmd(nc, [arrays], core_ids=[0])
    return r.results[0]["out_0"].reshape(NB, T, D)
```

```python
from contextlib import ExitStack

import numpy as np

import concourse.bass as bass
from concourse import mybir

ALU = mybir.AluOpType
ACT = mybir.ActivationFunctionType
F32 = mybir.dt.float32
BF16 = mybir.dt.bfloat16
AX_X = mybir.AxisListType.X

P = 128
NB, T, D = 8, 1024, 128
NH, HD = 8, 16
WIN, TOPK = 64, 32
RANK = 4
NE, ER = 8, 64
NR, NG = 4, 2
TP = T + WIN
CH = P
NCH = NB * T // CH
CPB = T // CH
HALF = 512
VD = HD + 1
SW = 3 * WIN + 2 * HD
BIG = 1e30
GONE = -1e4
EPS_LN = 1e-5
GATE2 = 0.2 * 0.2

C_ID = 0
C_MASK = C_ID + P
C_UNF = C_MASK + SW
C_ROW = C_UNF + 2 * WIN
C_SELN = C_ROW + 3
C_SELQ = C_SELN + NG * NH
C_SELE = C_SELQ + NR * HD
C_BLK = C_SELE + HD
C_EXP = C_BLK + NG * NR
C_END = C_EXP + NE * ER


def constants():
    c = np.zeros((P, C_END), np.float32)
    c[:, C_ID:C_ID + P] = np.eye(P, dtype=np.float32)
    i = (np.arange(P) % WIN)[:, None]
    late = (np.arange(P) >= WIN)[:, None]
    j = np.arange(WIN)[None, :]
    own = np.where(j > i, BIG, np.where(j == i, -BIG, 0.0))
    before = np.where(j > i, 0.0, BIG)
    none = np.zeros_like(own)
    first, middle, last = np.where(late, none, before), np.where(late, before, own), np.where(late, own, none)
    c[:, C_MASK:C_MASK + 3 * WIN] = np.concatenate([first, middle, last], 1)
    c[:, C_UNF:C_UNF + 2 * WIN] = np.concatenate([np.where(late, middle, first), np.where(late, last, middle)], 1) <= 0
    e = np.arange(P) % 32
    r = np.arange(P) // 32
    c[:, C_ROW] = np.where(e < HD, -2.0, 0.0)
    c[:, C_ROW + 1] = e == HD + 1
    c[:, C_ROW + 2] = (e == HD) | (e == HD + 1)
    for p in range(P):
        if e[p] < HD:
            for g in range(NG):
                c[p, C_SELN + g * NH + NG * r[p] + g] = -0.5
            c[p, C_SELQ + r[p] * HD + e[p]] = 1.0
            c[p, C_SELE + e[p]] = 1.0
    for h in range(NH):
        c[h * RANK:(h + 1) * RANK, C_BLK + (h % NG) * NR + h // NG] = 1.0
    for x in range(NE):
        c[x, C_EXP + x * ER:C_EXP + (x + 1) * ER] = 1.0
    return c


def adaln_block(nc, x, encq, encv, w1, b1, w2, b2, base, hebu, hebv, dec, wr, amat, bmat, cin, wmod, consts, out):
    ctx = ExitStack()

    def sb(name, shape, dt=F32):
        return ctx.enter_context(nc.sbuf_tensor(name, shape, dt))

    def sem(name):
        return ctx.enter_context(nc.semaphore(name))

    with ctx:
        con = sb("con", [P, C_END])
        encq_sb = sb("encq_sb", [P, NG, P])
        encv_sb = sb("encv_sb", [P, P])
        w1_sb = sb("w1_sb", [P, NG, 64])
        b1_sb = sb("b1_sb", [64, 1])
        w2_sb = sb("w2_sb", [64, NG, P])
        b2_sb = sb("b2_sb", [P, NG])
        base_sb = sb("base_sb", [P, NG])
        hebu_sb = sb("hebu_sb", [NH * RANK, HD])
        hebv_sb = sb("hebv_sb", [NH * RANK, HD])
        dec_sb = sb("dec_sb", [P, D])
        wr_sb = sb("wr_sb", [P, NE])
        a_sb = sb("a_sb", [P, 4, D])
        b_sb = sb("b_sb", [P, 4, D])
        c_sb = sb("c_sb", [P, NB])
        wmod_sb = sb("wmod_sb", [P, 6 * D])
        x0_sb = sb("x0_sb", [NB, D])
        ident = con[:, C_ID:C_ID + P]
        seln = con[:, C_SELN:C_SELN + NG * NH].rearrange("p (g h) -> p g h", g=NG)
        unf = con[:, C_UNF:C_UNF + 2 * WIN].rearrange("p (v j) -> p v j", v=2)
        ident_bf = sb("ident_bf", [P, P], BF16)
        mask_bf = sb("mask_bf", [P, SW], BF16)
        bias = sb("bias", [P, 4])
        hT_all = sb("hT_all", [P, NB * TP])
        qT_all = sb("qT_all", [P, NG, NB * TP])
        dec_b = sb("dec_b", [P, NB, D])
        g_b = sb("g_b", [P, NB, D])
        selheb = sb("selheb", [P, NG, 2, NR * HD])
        aS = sb("aS", [P, NG, NB])
        modT = sb("modT", [P, 6, NB])
        ec = sb("ec", [P, NB])
        sil = sb("sil", [P, NB])
        modn = sb("modn", [NB, 6 * D])
        gn = sb("gn", [NB, 2, D])
        gsgn = sb("gsgn", [NB, 2, D])
        gabs = sb("gabs", [NB, 2, D])
        udiag = sb("udiag", [NH * RANK, NG, NR, 32])
        vdiag = sb("vdiag", [NH * RANK, NG, NR, HD])
        key = sb("key", [P, 2, NH * WIN])
        big = sb("big", [P, 2, 2, NH * CH])
        xp = big[:, 0].rearrange("p s (u c d) -> p (s u) c d", u=2, c=4)
        xn = key[:].rearrange("p h (c d) -> p h c d", c=4)
        st_p = sb("st_p", [P, 4, 4, 6])
        mv_p = sb("mv_p", [P, 4, 4, 2])
        rs_p = sb("rs_p", [P, 4, 4])
        qsum = sb("qsum", [P, NG, 2, NB])
        qsum8 = sb("qsum8", [P, NG, NB])
        sig = sb("sig", [P, NG, NB])
        h1 = sb("h1", [64, NB])
        sp = sb("sp", [P, 8, NG * NB])
        z8 = sb("z8", [NB, 9, P])
        s8 = sb("s8", [NB, 24, 8])
        o0T = sb("o0T", [P, NB])
        h0T = sb("h0T", [P, NB])
        gateT = sb("gateT", [NE, NB])
        mI = sb("mI", [P, 4, D])
        gate_er = sb("gate_er", [P, 4, NB])
        bsc = big[:].rearrange("p a s (b d) -> p (a s) b d", b=NB)
        hst = sb("hst", [P, 2, 3 * WIN])
        tst = sb("tst", [P, 2, NR, NG, CH])
        one_row = sb("one_row", [1, 2 * NG * CH])
        sst = sb("sst", [P, 2, NG, SW])
        sqs = sb("sqs", [P, 2, NG, 3 * WIN])
        nst = sb("nst", [NH, 2, 3 * WIN])
        work = sb("work", [P, 2, NH * WIN])
        m8 = sb("m8", [P, NH, 8])
        wun = big[:, 0].rearrange("p s (h j) -> p s h j", h=NH)
        wts = big[:, 1].rearrange("p s (h t) -> p s h t", h=NH)
        vst = sb("vst", [P, 4, NH, 2, VD])
        qh = sb("qh", [P, 4, NH, 2 * HD])
        cst = sb("cst", [P, 2, NH, VD])
        den = sb("den", [P, 2, NH])
        rden = sb("rden", [P, 2, NH])
        selm = sb("selm", [P, 2, NG, NH])
        n2 = sb("n2", [P, 4, NH])
        n2g = sb("n2g", [P, 4, NH])
        lnn = sb("lnn", [P, NH])
        rnn = sb("rnn", [P, 2, NH])
        gat = sb("gat", [P, 4, NH])
        hsc = sb("hsc", [P, NH])
        t1 = sb("t1", [P, NH * HD])
        t2 = sb("t2", [P, NH * HD])
        osp = sb("osp", [P, 2, NH * HD])
        oT = sb("oT", [P, 2, CH])
        xs = sb("xs", [P, 4, D])
        x2 = sb("x2", [P, 2, D])
        st_c = sb("st_c", [P, 6])
        mv_c = sb("mv_c", [P, 2, 2])
        lv_c = sb("lv_c", [P, 1])
        nm_c = sb("nm_c", [P, 1])
        nb_c = sb("nb_c", [P, 1])
        rs_c = sb("rs_c", [P, 2])
        n_c = sb("n_c", [P, 2, D])
        h2T = sb("h2T", [P, 2, CH])
        yo = sb("yo", [P, 2, D])

        psD = ctx.enter_context(nc.psum_tensor("psD", [P, 4, 512], F32))
        psW = ctx.enter_context(nc.psum_tensor("psW", [P, 2, 512], F32))
        psC = ctx.enter_context(nc.psum_tensor("psC", [P, 512], F32))
        psX = ctx.enter_context(nc.psum_tensor("psX", [P, 512], F32))
        pH = psD[:].rearrange("p r (g x) -> p (r g) x", g=NG)
        pQH = pH[:, :, 3 * WIN:SW]
        pV = psW[:, 1, 0:2 * P].rearrange("p (v x) -> p v x", v=2)
        pC = psC[:, 0:NH * 2 * VD]
        pO = psX[:, 2 * P:3 * P]
        pAtt = psX[:, 3 * P:4 * P]
        pN2 = psX[:, 0:P]
        pY = psX[:, P:2 * P]
        pN = psW[0:NH, 0, 0:3 * WIN]
        pNN = psW[:, 0, 3 * WIN:3 * WIN + NH]

        con_in = sem("con_in")
        c_in = sem("c_in")
        wq_in = sem("wq_in")
        wts_in = sem("wts_in")
        bias_set = sem("bias_set")
        bf_set = sem("bf_set")
        ec_ready = sem("ec_ready")
        sil_ready = sem("sil_ready")
        pmod_ready = sem("pmod_ready")
        modT_ready = sem("modT_ready")
        modn_ready = sem("modn_ready")
        dve_chain = sem("dve_chain")
        pool_chain = sem("pool_chain")
        gates_n_ready = sem("gates_n_ready")
        pgate_ready = sem("pgate_ready")
        diag_ready = sem("diag_ready")
        pheb_ready = sem("pheb_ready")
        selheb_ready = sem("selheb_ready")
        xp_in = [sem(f"xp_in{i}") for i in range(4)]
        mv_ready = sem("mv_ready")
        lnv_p = sem("lnv_p")
        rs_ready = sem("rs_ready")
        st_ready = sem("st_ready")
        xn_ready = sem("xn_ready")
        pT_ready = sem("pT_ready")
        hT_ready = sem("hT_ready")
        pq_ready = sem("pq_ready")
        q_ready = sem("q_ready")
        qsum8_ready = sem("qsum8_ready")
        pads_ready = sem("pads_ready")
        sig_ready = sem("sig_ready")
        pm1_ready = sem("pm1_ready")
        h1_ready = sem("h1_ready")
        pm2_ready = sem("pm2_ready")
        z_ready = sem("z_ready")
        sp_act = sem("sp_act")
        sp_dve = sem("sp_dve")
        aS_ready = sem("aS_ready")
        p0_ready = sem("p0_ready")
        r0_act = sem("r0_act")
        r0_dve = sem("r0_dve")
        r0_pe = sem("r0_pe")
        bsc_ready = sem("bsc_ready")
        pG_ready = sem("pG_ready")
        gatew_ready = sem("gatew_ready")
        gb_ready = sem("gb_ready")
        ones_set = sem("ones_set")
        ones_in = sem("ones_in")
        waits_alone = sem("waits_alone")
        opnd_ready = sem("opnd_ready")
        pn_ready = sem("pn_ready")
        nst_ready = sem("nst_ready")
        rows_in = [sem("rows_in0"), sem("rows_in1")]
        dist_ready = sem("dist_ready")
        v_ready = sem("v_ready")
        outer_ready = sem("outer_ready")
        d2_ready = sem("d2_ready")
        ln_done = sem("ln_done")
        key_ready = sem("key_ready")
        vst_ready = sem("vst_ready")
        qhs_ready = sem("qhs_ready")
        picked = sem("picked")
        square_done = sem("square_done")
        wsel_ready = sem("wsel_ready")
        w_ready = sem("w_ready")
        wt_ready = sem("wt_ready")
        wts_ready = sem("wts_ready")
        c_ready = sem("c_ready")
        cst_ready = sem("cst_ready")
        den_done = sem("den_done")
        rden_ready = sem("rden_ready")
        nm_done = sem("nm_done")
        nb_done = sem("nb_done")
        rs_done = sem("rs_done")
        n2_ready = sem("n2_ready")
        n2g_ready = sem("n2g_ready")
        lnn_done = sem("lnn_done")
        rnn_ready = sem("rnn_ready")
        mix_step = sem("mix_step")
        osp_ready = sem("osp_ready")
        po_ready = sem("po_ready")
        oT_ready = sem("oT_ready")
        att_ready = sem("att_ready")
        xs_in = [sem(f"xs_in{i}") for i in range(4)]
        x2_ready = sem("x2_ready")
        stc_ready = sem("stc_ready")
        mvc_ready = sem("mvc_ready")
        lnc_done = sem("lnc_done")
        nc_ready = sem("nc_ready")
        pn2_ready = sem("pn2_ready")
        h2T_ready = sem("h2T_ready")
        y_ready = sem("y_ready")
        yo_ready = sem("yo_ready")
        out_in = [sem("out_in0"), sem("out_in1")]

        def need(eng, s, value):
            if isinstance(value, int) and value <= 0:
                return
            eng.wait_ge(s, value)

        def wait_alone(eng, s, value):
            if isinstance(value, int) and value <= 0:
                return
            eng.wait_ge(s, value)
            if not isinstance(value, int):
                eng.sem_inc(waits_alone, 1)

        ROWS_IN = 16 * (1 + NR + NG + NR)
        FIRST, LAST = -3, NCH + 2
        LOOP0, LOOP1, UNROLL = 5, 58, 4

        def steps(eng, step, routing=None):
            for i in range(FIRST, LOOP0):
                if routing and i <= 1:
                    routing(i)
                step(i, i % UNROLL)
            with eng.Fori(LOOP0, LOOP1, UNROLL) as i0:
                for u in range(UNROLL):
                    step(i0 + u, (LOOP0 + u) % UNROLL)
            for i in range(LOOP1 + UNROLL - 1, LAST + 1):
                step(i, i % UNROLL)

        def there(i, off):
            return not isinstance(i, int) or 0 <= i + off < NCH

        def column(k):
            return k * CH + (k // CPB) * WIN

        block = ctx.enter_context(nc.Block())

        @block.sync
        def _(sync):
            xh = x.rearrange("(n c p) d -> p n c d", c=4, p=P)
            for n in range(2):
                sync.dma_start(xp[:, n], xh[:, n]).then_inc(xp_in[n], 16)
            sync.dma_start(c_sb[:], cin).then_inc(c_in, 16)
            sync.dma_start(wmod_sb[:], wmod).then_inc(c_in, 16)
            sync.dma_start(con[:], consts).then_inc(con_in, 16)
            sync.dma_start(encq_sb[:], encq).then_inc(wq_in, 16)
            for n in range(2, 4):
                sync.dma_start(xp[:, n], xh[:, n]).then_inc(xp_in[n], 16)
            for dst, src in ((encv_sb, encv), (w1_sb, w1), (b1_sb, b1), (w2_sb, w2), (b2_sb, b2), (base_sb, base),
                             (hebu_sb, hebu), (hebv_sb, hebv), (dec_sb, dec), (wr_sb, wr), (a_sb, amat), (b_sb, bmat)):
                sync.dma_start(dst[:], src).then_inc(wts_in, 16)
            sync.dma_start(x0_sb[:], x.rearrange("(b t) d -> b t d", b=NB)[:, 0, :]).then_inc(wts_in, 16)
            with sync.Fori(4, 2 * NB - 3, 4) as n0:
                for u in range(4):
                    sync.wait_ge(xn_ready, n0 - 3 + u)
                    sync.dma_start(xp[:, u], xh[:, bass.ds(n0 + u, 1)].squeeze(1)).then_inc(xp_in[u], 16)

            xc = x.rearrange("(n p) d -> p n d", p=P)
            oc = out.rearrange("(n p) d -> p n d", p=P)

            def step(i, ph):
                k = i - 3
                if there(i, -3):
                    s = (ph - 3) % 2
                    sync.wait_ge(yo_ready, k + 1)
                    sync.dma_start(oc[:, bass.ds(k, 1)].squeeze(1), yo[:, s]).then_inc(out_in[s], 16)
                k, s = i + 3, (ph + 3) % 2
                if there(i, 3):
                    c0 = column(k)
                    need(sync, dist_ready, k - 1)
                    sync.dma_start(hst[:, s], hT_all[:, bass.ds(c0, 3 * WIN)]).then_inc(rows_in[s], 16)
                    for r in range(NR):
                        rows = slice(32 * r, 32 * r + HD)
                        sync.dma_start(tst[rows, s, r], qT_all[rows, :, bass.ds(c0 + WIN, CH)]).then_inc(rows_in[s], 16)
                    sync.wait_ge(nst_ready, k + 1)
                    for g in range(NG):
                        sync.dma_start(sst[HD:P:32, s, g, 0:3 * WIN], nst[g:NH:NG, s]).then_inc(rows_in[s], 16)
                    for r in range(NR):
                        sync.dma_start(tst[32 * r + HD + 1:32 * r + HD + 2, s, r],
                                       nst[NG * r:NG * (r + 1), s, WIN:3 * WIN]).then_inc(rows_in[s], 16)
                k = i + 1
                if there(i, 1):
                    need(sync, att_ready, k - 3)
                    sync.dma_start(xs[:, (ph + 1) % 4], xc[:, bass.ds(k, 1)].squeeze(1)).then_inc(xs_in[(ph + 1) % 4], 16)

            sync.wait_ge(ones_set, 7)
            for r in range(NR):
                sync.dma_start(tst[32 * r + HD:32 * r + HD + 1, :, r],
                               one_row[:].rearrange("p (s g t) -> p s g t", s=2, g=NG)).then_inc(ones_in, 16)
            sync.wait_ge(pads_ready, 2 * NB)
            sync.wait_ge(q_ready, 4 * NB)
            sync.wait_ge(hT_ready, 2 * NB)
            steps(sync, step)
            for s in range(2):
                sync.wait_ge(out_in[s], 16 * NCH // 2)

        @block.gpsimd
        def _(pool):
            links = [0]

            def link(ins):
                links[0] += 1
                ins.then_inc(pool_chain, 1)
                pool.wait_ge(pool_chain, links[0])

            for col, value in enumerate((EPS_LN, 1e-8, 1.0, 0.0)):
                nc.gpsimd.memset(bias[:, col:col + 1], value).then_inc(bias_set, 1)
            nc.gpsimd.memset(udiag[:], 0.0).then_inc(ones_set, 1)
            for s in range(4):
                nc.gpsimd.memset(vst[:, s, :, :, HD:VD], 1.0).then_inc(ones_set, 1)
            nc.gpsimd.memset(one_row[:], 1.0).then_inc(ones_set, 1)
            nc.gpsimd.memset(tst[:], 0.0).then_inc(ones_set, 1)
            pool.wait_ge(con_in, 16)
            nc.gpsimd.tensor_copy(sst[:, :, :, 3 * WIN:3 * WIN + HD].rearrange("p s g e -> p (s g) e"),
                                  con[:, C_SELE:C_SELE + HD].unsqueeze(1).broadcast_to([P, 2 * NG, HD])).then_inc(ones_set, 1)
            nc.gpsimd.tensor_copy(ident_bf[:], ident).then_inc(bf_set, 1)
            nc.gpsimd.tensor_copy(mask_bf[:], con[:, C_MASK:C_MASK + SW]).then_inc(bf_set, 1)
            pool.wait_ge(wts_in, 16 * 13)
            pool.wait_ge(ones_set, 1)
            hk = NH * RANK
            for g in range(NG):
                blk = con[0:hk, C_BLK + g * NR:C_BLK + (g + 1) * NR].unsqueeze(2).broadcast_to([hk, NR, HD])
                for dst, src in ((udiag[:, g, :, 0:HD], hebu_sb), (vdiag[:, g], hebv_sb)):
                    nc.gpsimd.tensor_tensor(dst, src[:].unsqueeze(1).broadcast_to([hk, NR, HD]), blk,
                                            ALU.mult).then_inc(diag_ready, 1)
            with pool.Fori(0, NB) as b:
                c0 = b * TP
                pool.wait_ge(hT_ready, 2 * b + 1)
                nc.gpsimd.tensor_copy(hT_all[:, bass.ds(c0, WIN)],
                                      hT_all[:, bass.ds(c0 + WIN, 1)].broadcast_to([P, WIN])).then_inc(pads_ready, 1)
                pool.wait_ge(q_ready, 4 * b + 2)
                nc.gpsimd.tensor_copy(qT_all[:, :, bass.ds(c0, WIN)],
                                      qT_all[:, :, bass.ds(c0 + WIN, 1)].broadcast_to([P, NG, WIN])).then_inc(pads_ready, 1)

            pool.wait_ge(pads_ready, 2 * NB)
            pool.wait_ge(q_ready, 4 * NB)

            def step(i, ph):
                k, s, s4 = i - 2, ph % 2, (ph - 2) % 4
                if there(i, -2):
                    q, hb = qh[:, s4, :, 0:HD], qh[:, s4, :, HD:2 * HD]
                    h3 = "p (h e) -> p h e"
                    pool.wait_ge(rnn_ready, k + 1)
                    nc.gpsimd.tensor_tensor(hsc[:], gat[:, s4], rnn[:, s], ALU.mult).then_inc(mix_step, 1)
                    pool.wait_ge(cst_ready, 2 * (k + 1))
                    nc.gpsimd.tensor_tensor(t1[:].rearrange(h3, h=NH), cst[:, s, :, 0:HD], q, ALU.mult).then_inc(mix_step, 1)
                    pool.wait_ge(mix_step, 5 * k + 1)
                    nc.gpsimd.tensor_tensor(t2[:].rearrange(h3, h=NH), hb, hsc[:].unsqueeze(2).broadcast_to([P, NH, HD]),
                                            ALU.mult).then_inc(mix_step, 1)
                    pool.wait_ge(mix_step, 5 * k + 3)
                    nc.gpsimd.tensor_tensor(t2[:].rearrange(h3, h=NH), t2[:].rearrange(h3, h=NH), q, ALU.mult).then_inc(mix_step, 1)
                    pool.wait_ge(rden_ready, k + 1)
                    nc.gpsimd.tensor_tensor(t1[:].rearrange(h3, h=NH), t1[:].rearrange(h3, h=NH),
                                            rden[:, s].unsqueeze(2).broadcast_to([P, NH, HD]), ALU.mult).then_inc(mix_step, 1)
                    need(pool, po_ready, k - 1)
                    pool.wait_ge(mix_step, 5 * k + 5)
                    nc.gpsimd.tensor_tensor(osp[:, s], t1[:], t2[:], ALU.add).then_inc(osp_ready, 1)
                k, s, s4 = i - 1, (ph - 1) % 2, (ph - 1) % 4
                if there(i, -1):
                    need(pool, wt_ready, 8 * (k - 1))
                    for w in range(2):
                        pool.wait_ge(wsel_ready, 2 * k + 1 + w)
                        heads = slice(4 * w, 4 * w + 4)
                        nc.gpsimd.tensor_tensor(
                            wun[:, s, heads].rearrange("p h (v j) -> p h v j", v=2),
                            work[:, s].rearrange("p (h j) -> p h j", h=NH)[:, heads].unsqueeze(2).broadcast_to([P, 4, 2, WIN]),
                            unf.unsqueeze(1).broadcast_to([P, 4, 2, WIN]), ALU.mult).then_inc(w_ready, 1)
                k, s = i + 3, (ph + 3) % 2
                if there(i, 3):
                    b, c0 = k // CPB, column(k)
                    win = qT_all[:, :, bass.ds(c0, 3 * WIN)]
                    wait_alone(pool, pn_ready, k - 1)
                    nc.gpsimd.tensor_tensor(sqs[:, s], win, win, ALU.mult).then_inc(opnd_ready, 1)
                    if isinstance(i, int) and i == FIRST:
                        pool.wait_ge(aS_ready, 1)
                    wait_alone(pool, dist_ready, k - 1)
                    nc.gpsimd.tensor_tensor(sst[:, s, :, 0:3 * WIN], win,
                                            aS[:, :, bass.ds(b, 1)].broadcast_to([P, NG, 3 * WIN]), ALU.mult).then_inc(opnd_ready, 1)
                    nc.gpsimd.tensor_tensor(selm[:, s], seln, aS[:, :, bass.ds(b, 1)].broadcast_to([P, NG, NH]),
                                            ALU.mult).then_inc(opnd_ready, 1)
                k, s4 = i + 1, (ph + 1) % 4
                if there(i, 1):
                    wait_alone(pool, n2_ready, k + 1)
                    wait_alone(pool, rnn_ready, k - 3)
                    nc.gpsimd.tensor_scalar(gat[:, s4], n2[:, s4], GATE2, 0.1, ALU.is_gt, ALU.mult).then_inc(n2g_ready, 1)
                    nc.gpsimd.tensor_scalar(n2g[:, s4], n2[:, s4], 1e-18, None, ALU.max).then_inc(n2g_ready, 1)

            def routing(i):
                if i == 0:
                    pool.wait_ge(r0_dve, 10)
                    for kt in range(2, 4):
                        nc.gpsimd.tensor_tensor(bsc[:, kt], b_sb[:, kt].unsqueeze(1).broadcast_to([P, NB, D]),
                                                gate_er[:, kt].unsqueeze(2).broadcast_to([P, NB, D]), ALU.mult).then_inc(bsc_ready, 1)
                if i == 1:
                    pool.wait_ge(pG_ready, 2)

            steps(pool, step, routing)

        @block.scalar
        def _(act):
            act.preload_act_table_set("natural_log_exp_and_others")
            act.wait_ge(c_in, 32)
            nc.scalar.activation(ec[:], c_sb[:], ACT.Exp, scale=-1.0).then_inc(ec_ready, 1)
            act.wait_ge(bias_set, 4)

            def logvar(n, u):
                act.wait_ge(mv_ready, 4 * n + 4)
                nc.scalar.activation(rs_p[:, u], mv_p[:, u, :, 1], ACT.Ln, bias=bias[:, 0:1]).then_inc(lnv_p, 1)

            def invstd(n, u):
                act.wait_ge(lnv_p, n + 1)
                nc.scalar.activation(rs_p[:, u], rs_p[:, u], ACT.Exp, scale=-0.5).then_inc(rs_ready, 1)

            for n in range(2):
                logvar(n, n)
                invstd(n, n)
            act.wait_ge(pmod_ready, 1)
            nc.scalar.activation(modT[:].rearrange("p j b -> p (j b)"), psC[:, 0:6 * NB], ACT.Copy).then_inc(modT_ready, 1)
            act.wait_ge(pmod_ready, 2)
            for j in range(2):
                nc.scalar.activation(modn[:, j * 384:(j + 1) * 384], psW[0:NB, j, 0:384], ACT.Copy).then_inc(modn_ready, 1)
            act.wait_ge(modT_ready, 2)
            act.wait_ge(con_in, 16)
            def columns(n):
                return bass.ds((n // 2) * TP + WIN + (n % 2) * HALF, HALF)

            def to_hT(n, u):
                b = n // 2
                act.wait_ge(pT_ready, n + 1)
                nc.scalar.activation(hT_all[:, columns(n)], psW[:, u % 2], ACT.Identity, bias=modT[:, 0, bass.ds(b, 1)],
                                     scale=modT[:, 1, bass.ds(b, 1)]).then_inc(hT_ready, 1)

            def to_q(n, u):
                for g in range(NG):
                    act.wait_ge(pq_ready, 2 * n + g + 1)
                    nc.scalar.activation(qT_all[:, g, columns(n)], psD[:, 2 * (u % 2) + g], ACT.Relu,
                                         bias=con[:, C_ROW + 2:C_ROW + 3],
                                         accum_out=qsum[:, g, u % 2, bass.ds(n // 2, 1)]).then_inc(q_ready, 1)

            to_hT(0, 0)
            act.wait_ge(pheb_ready, 2)
            for g in range(NG):
                nc.scalar.activation(selheb[:, g, 1], psX[:, 256 + g * 64:320 + g * 64], ACT.Copy).then_inc(selheb_ready, 1)
            for s in range(2):
                nc.scalar.activation(sst[:, s, :, 3 * WIN + HD:SW], psX[:, 384:384 + NG * HD].rearrange("p (g e) -> p g e", g=NG),
                                     ACT.Copy).then_inc(selheb_ready, 1)
            logvar(2, 2)
            invstd(2, 2)
            with act.Fori(0, 2 * NB - 7, 4) as n0:
                for u in range(4):
                    logvar(n0 + u + 3, (u + 3) % 4)
                    to_hT(n0 + u + 1, (u + 1) % 4)
                    invstd(n0 + u + 3, (u + 3) % 4)
                    to_q(n0 + u, u)
            for n in range(2 * NB - 4, 2 * NB):
                if n + 3 < 2 * NB:
                    logvar(n + 3, (n + 3) % 4)
                if n + 1 < 2 * NB:
                    to_hT(n + 1, (n + 1) % 4)
                if n + 3 < 2 * NB:
                    invstd(n + 3, (n + 3) % 4)
                to_q(n, n % 4)
            act.wait_ge(pm1_ready, 1)
            nc.scalar.activation(h1[:], psX[0:64, 0:NB], ACT.Gelu, bias=b1_sb[:]).then_inc(h1_ready, 1)
            act.wait_ge(p0_ready, 1)
            nc.scalar.activation(z8[:, 0:2].rearrange("p a b -> p (a b)"), psW[0:NB, 1, 0:256], ACT.Copy).then_inc(r0_act, 1)
            nc.scalar.activation(z8[:, 2], psW[0:NB, 1, 256:384], ACT.Relu).then_inc(r0_act, 1)
            act.preload_act_table_set("natural_log_exp_and_others")
            act.wait_ge(z_ready, 1)
            nc.scalar.activation(sp[:, 1], sp[:, 0], ACT.Abs).then_inc(sp_act, 1)
            act.wait_ge(sp_act, 1)
            nc.scalar.activation(sp[:, 2], sp[:, 1], ACT.Exp, scale=-1.0).then_inc(sp_act, 1)
            act.wait_ge(r0_dve, 1)
            nc.scalar.activation(s8[:, 2], s8[:, 1], ACT.Ln).then_inc(r0_act, 1)
            act.wait_ge(r0_act, 3)
            nc.scalar.activation(s8[:, 3], s8[:, 2], ACT.Exp, scale=-0.5).then_inc(r0_act, 1)
            act.wait_ge(sp_dve, 1)
            nc.scalar.activation(sp[:, 4], sp[:, 3], ACT.Ln).then_inc(sp_act, 1)

            def routing(i):
                if i == -2:
                    act.wait_ge(r0_dve, 4)
                    nc.scalar.activation(s8[:, 7, 0:1], s8[:, 6, 1:2], ACT.Ln, bias=bias[0:NB, 0:1]).then_inc(r0_act, 1)
                    act.wait_ge(r0_act, 5)
                    nc.scalar.activation(s8[:, 7, 1:2], s8[:, 7, 0:1], ACT.Exp, scale=-0.5).then_inc(r0_act, 1)
                    act.wait_ge(r0_dve, 7)
                    nc.scalar.activation(s8[:, 11], s8[:, 8], ACT.Exp, bias=s8[:, 10, 0:1]).then_inc(r0_act, 1)

            def step(i, ph):
                def weights(w):
                    if there(i, -1):
                        wk = work[:, (ph - 1) % 2, w * 4 * WIN:(w + 1) * 4 * WIN]
                        act.wait_ge(picked, 16 * (i - 1) + 15 + w)
                        nc.scalar.activation(wk, wk, ACT.Square).then_inc(square_done, 1)
                        act.wait_ge(square_done, 2 * (i - 1) + 1 + w)
                        nc.scalar.activation(wk, wk, ACT.Exp, scale=-1.0).then_inc(wsel_ready, 1)

                weights(0)
                k, s = i - 3, (ph - 3) % 2
                if there(i, -3):
                    act.wait_ge(nm_done, k + 1)
                    act.wait_ge(rs_done, k + 1)
                    nc.scalar.activation(nb_c[:], nm_c[:], ACT.Identity, bias=bias[:, 3:4], scale=rs_c[:, s:s + 1]).then_inc(nb_done, 1)
                weights(1)
                if there(i, -2):
                    act.wait_ge(po_ready, i - 1)
                    nc.scalar.activation(oT[:, ph % 2], pO, ACT.Copy).then_inc(oT_ready, 1)
                if there(i, -3):
                    act.wait_ge(nb_done, k + 1)
                    need(act, pn2_ready, k - 1)
                    nc.scalar.activation(n_c[:, s], x2[:, s], ACT.Identity, bias=nb_c[:], scale=rs_c[:, s:s + 1]).then_inc(nc_ready, 1)
                k, s, s4 = i + 1, (ph + 1) % 2, (ph + 1) % 4
                if there(i, 1):
                    act.wait_ge(dist_ready, k + 1)
                    need(act, picked, 16 * (k - 2) + 4)
                    e = key[:, s].rearrange("p (h j) -> p h j", h=NH)
                    nc.scalar.activation(e[0:WIN], pH[0:WIN, :, 0:WIN], ACT.Relu).then_inc(outer_ready, 1)
                    nc.scalar.activation(e[WIN:P], pH[WIN:P, :, 2 * WIN:3 * WIN], ACT.Relu).then_inc(outer_ready, 1)
                if there(i, -2):
                    act.wait_ge(att_ready, i - 1)
                    nc.scalar.activation(x2[:, ph % 2], pAtt, ACT.Copy).then_inc(x2_ready, 1)

                def to_wts(w):
                    if there(i, -1):
                        act.wait_ge(wt_ready, 8 * (i - 1) + 4 * w + 4)
                        need(act, c_ready, i - 2)
                        nc.scalar.activation(wts[:, (ph - 1) % 2, 4 * w:4 * w + 4].rearrange("p h t -> p (h t)"), psW[:, w],
                                             ACT.Copy).then_inc(wts_ready, 1)

                to_wts(0)
                k, s, s4 = i + 1, (ph + 1) % 2, (ph + 1) % 4
                if there(i, 1):
                    need(act, osp_ready, k - 3)
                    nc.scalar.activation(qh[:, s4], pQH, ACT.Copy).then_inc(qhs_ready, 1)
                to_wts(1)
                k, s = i - 3, (ph - 3) % 2
                if there(i, -3):
                    b = k // CPB
                    act.wait_ge(pn2_ready, k + 1)
                    need(act, y_ready, k - 1)
                    nc.scalar.activation(h2T[:, s], pN2, ACT.Identity, bias=modT[:, 3, bass.ds(b, 1)],
                                         scale=modT[:, 4, bass.ds(b, 1)]).then_inc(h2T_ready, 1)
                k, s = i + 1, (ph + 1) % 2
                if there(i, 1):
                    act.wait_ge(d2_ready, k + 1)
                    nc.scalar.activation(key[:, s], key[:, s], ACT.Ln, bias=bias[:, 1:2]).then_inc(ln_done, 1)
                    act.wait_ge(ln_done, k + 1)
                    nc.scalar.activation(key[:, s], key[:, s], ACT.Exp, scale=0.25).then_inc(key_ready, 1)
                k, s = i - 1, (ph - 1) % 2
                if there(i, -1):
                    act.wait_ge(c_ready, k + 1)
                    need(act, osp_ready, k - 1)
                    pc = pC.rearrange("p (h v e) -> p h v e", h=NH, v=2)
                    nc.scalar.activation(cst[0:WIN, s], pc[0:WIN, :, 0], ACT.Copy).then_inc(cst_ready, 1)
                    nc.scalar.activation(cst[WIN:P, s], pc[WIN:P, :, 1], ACT.Copy).then_inc(cst_ready, 1)
                k, s = i - 3, (ph - 3) % 2
                if there(i, -3):
                    act.wait_ge(y_ready, k + 1)
                    need(act, out_in[s], 16 * (k // 2))
                    nc.scalar.activation(yo[:, s], pY, ACT.Copy).then_inc(yo_ready, 1)
                k, s, s4 = i - 1, (ph - 1) % 2, (ph - 1) % 4
                if there(i, -1):
                    act.wait_ge(n2g_ready, 2 * (k + 1))
                    nc.scalar.activation(lnn[:], n2g[:, s4], ACT.Ln).then_inc(lnn_done, 1)
                    act.wait_ge(lnn_done, k + 1)
                    nc.scalar.activation(rnn[:, s], lnn[:], ACT.Exp, scale=-0.5).then_inc(rnn_ready, 1)
                k, s, s4 = i + 3, (ph + 3) % 2, (ph + 3) % 4
                if there(i, 3):
                    act.wait_ge(pn_ready, k + 1)
                    need(act, n2g_ready, 2 * (k - 3))
                    nc.scalar.activation(n2[:, s4], pNN, ACT.Copy, scale=-2.0).then_inc(n2_ready, 1)
                    need(act, rows_in[s], ROWS_IN * (k // 2))
                    nc.scalar.activation(nst[:, s], pN, ACT.Copy).then_inc(nst_ready, 1)
                k, s4 = i + 2, (ph + 2) % 4
                if there(i, 2):
                    act.wait_ge(v_ready, k + 1)
                    need(act, c_ready, k - 3)
                    nc.scalar.activation(vst[:, s4, :, :, 0:HD], pV.rearrange("p v (h e) -> p h v e", h=NH),
                                         ACT.Relu).then_inc(vst_ready, 1)
                k, s = i - 2, ph % 2
                if there(i, -2):
                    act.wait_ge(mvc_ready, k + 1)
                    nc.scalar.activation(lv_c[:], mv_c[:, s, 1:2], ACT.Ln, bias=bias[:, 0:1]).then_inc(lnc_done, 1)
                    nc.scalar.activation(nm_c[:], mv_c[:, s, 0:1], ACT.Copy, scale=-1.0).then_inc(nm_done, 1)
                    act.wait_ge(lnc_done, k + 1)
                    nc.scalar.activation(rs_c[:, s:s + 1], lv_c[:], ACT.Exp, scale=-0.5).then_inc(rs_done, 1)

            steps(act, step, routing)

        @block.vector
        def _(dve):
            links = [0]

            def link(ins):
                links[0] += 1
                ins.then_inc(dve_chain, 1)
                dve.wait_ge(dve_chain, links[0])

            v = nc.vector
            def stats(n, u):
                dve.wait_ge(xp_in[u], 16 * (n // 4) + 16)
                for c in range(4):
                    v.bn_stats(st_p[:, u, c], xp[:, u, c]).then_inc(st_ready, 1)
                for c in range(4):
                    wait_alone(dve, st_ready, 4 * n + c + 1)
                    v.bn_aggr(mv_p[:, u, c], st_p[:, u, c]).then_inc(mv_ready, 1)

            def normalise(n, u):
                dve.wait_ge(rs_ready, n + 1)
                need(dve, pT_ready, n - 1)
                for c in range(4):
                    last = v.tensor_scalar(xn[:, u % 2, c], xp[:, u, c], mv_p[:, u, c, 0:1],
                                           rs_p[:, u, c:c + 1], ALU.subtract, ALU.mult)
                last.then_inc(xn_ready, 1)

            def every_8th(b):
                dve.wait_ge(q_ready, 4 * b + 4)
                v.tensor_reduce(qsum8[:, :, bass.ds(b, 1)], qT_all[:, :, bass.ds(b * TP + WIN, T // 8, step=8)],
                                AX_X, ALU.add).then_inc(qsum8_ready, 1)

            stats(0, 0)
            dve.wait_ge(ec_ready, 1)
            link(v.tensor_scalar(ec[:], ec[:], 1.0, None, ALU.add))
            link(v.reciprocal(ec[:], ec[:]))
            v.tensor_tensor(sil[:], c_sb[:], ec[:], ALU.mult).then_inc(sil_ready, 1)
            stats(1, 1)
            dve.wait_ge(modT_ready, 1)
            for j in (1, 4):
                last = v.tensor_scalar(modT[:, j], modT[:, j], 1.0, None, ALU.add)
            last.then_inc(modT_ready, 1)
            normalise(0, 0)
            normalise(1, 1)
            stats(2, 2)
            stats(3, 3)
            dve.wait_ge(modn_ready, 2)
            gview = modn[:].rearrange("b (u v d) -> b u v d", u=2, v=3)[:, :, 2]
            link(v.tensor_scalar(gsgn[:], gview, 0.0, 2.0, ALU.is_ge, ALU.mult))
            link(v.tensor_scalar(gabs[:], gview, -1.0, None, ALU.mult))
            link(v.tensor_tensor(gabs[:], gabs[:], gview, ALU.max))
            link(v.tensor_scalar(gabs[:], gabs[:], 0.25, None, ALU.max))
            v.scalar_tensor_tensor(out=gn[:], in0=gsgn[:], scalar=-1.0, in1=gabs[:], op0=ALU.add,
                                   op1=ALU.mult).then_inc(gates_n_ready, 1)
            dve.wait_ge(con_in, 16)
            for g in range(NG):
                v.tensor_copy(selheb[:, g, 0], con[:, C_SELQ:C_SELQ + NR * HD]).then_inc(selheb_ready, 1)
            for n in range(2, 4):
                stats(n + 2, (n + 2) % 4)
                normalise(n, n)
            with dve.Fori(4, 2 * NB - 7, 4) as n0:
                for u in range(4):
                    n = n0 + u
                    stats(n + 2, (u + 2) % 4)
                    normalise(n, u)
                    if u % 2 == 0:
                        every_8th((n0 - 4 + u) // 2)
            for n in range(2 * NB - 4, 2 * NB):
                if n + 2 < 2 * NB:
                    stats(n + 2, (n + 2) % 4)
                normalise(n, n % 4)
            for b in range(NB - 4, NB):
                every_8th(b)
            link(v.tensor_tensor(sig[:], qsum[:, :, 0], qsum[:, :, 1], ALU.add))
            link(v.tensor_scalar(sig[:], sig[:], 1.0 / T, None, ALU.mult))
            dve.wait_ge(qsum8_ready, NB)
            v.scalar_tensor_tensor(out=sig[:], in0=qsum8[:], scalar=0.5 * 8 / T, in1=sig[:], op0=ALU.mult,
                                   op1=ALU.add).then_inc(sig_ready, 1)

            def gate_weights(pr):
                dve.wait_ge(pgate_ready, pr + 1)
                two = slice(2 * pr, 2 * pr + 2)
                gate_ps = psC[:].rearrange("p (b u d) -> p b u d", b=2, u=2)
                v.tensor_tensor(dec_b[:, two], dec_sb[:].unsqueeze(1).broadcast_to([P, 2, D]), gate_ps[:, :, 0], ALU.mult)
                v.tensor_copy(g_b[:, two], gate_ps[:, :, 1]).then_inc(gatew_ready, 1)

            dve.wait_ge(wts_in, 16 * 13)
            gate_weights(0)
            dve.wait_ge(pm2_ready, 1)
            z = sp[:, 0].rearrange("p (g b) -> p g b", g=NG)
            for g in range(NG):
                link(v.tensor_scalar(z[:, g], psX[:, 64 + g * NB:64 + (g + 1) * NB], b2_sb[:, g:g + 1], 0.1, ALU.add, ALU.mult))
            for g in range(NG):
                last = v.tensor_scalar(z[:, g], z[:, g], base_sb[:, g:g + 1], None, ALU.add)
            last.then_inc(z_ready, 1)
            gate_weights(1)
            q0, hb0, v0 = z8[:, 0], z8[:, 1], z8[:, 2]
            h3 = "p (h e) -> p h e"
            dve.wait_ge(r0_act, 2)
            link(v.tensor_tensor(z8[:, 3], q0, q0, ALU.mult))
            link(v.tensor_reduce(s8[:, 0], z8[:, 3].rearrange(h3, h=NH), AX_X, ALU.add))
            v.tensor_scalar(s8[:, 1], s8[:, 0], 1e-18, None, ALU.max).then_inc(r0_dve, 1)
            link(v.tensor_scalar(s8[:, 4], s8[:, 0], GATE2, 0.1, ALU.is_gt, ALU.mult))
            dve.wait_ge(sp_act, 2)
            v.tensor_scalar(sp[:, 3], sp[:, 2], 1.0, None, ALU.add).then_inc(sp_dve, 1)
            dve.wait_ge(sp_dve, 1)
            link(v.tensor_scalar(sp[:, 5], sp[:, 3], -1.0, None, ALU.add))
            link(v.tensor_scalar(sp[:, 6], sp[:, 5], 0.0, None, ALU.is_equal))
            link(v.tensor_tensor(sp[:, 5], sp[:, 5], sp[:, 6], ALU.add))
            link(v.reciprocal(sp[:, 5], sp[:, 5]))
            dve.wait_ge(sp_act, 3)
            link(v.tensor_tensor(sp[:, 6], sp[:, 6], sp[:, 4], ALU.add))
            link(v.tensor_tensor(sp[:, 6], sp[:, 6], sp[:, 5], ALU.mult))
            link(v.tensor_tensor(sp[:, 6], sp[:, 6], sp[:, 2], ALU.mult))
            link(v.scalar_tensor_tensor(out=sp[:, 7], in0=sp[:, 0], scalar=0.0, in1=sp[:, 6], op0=ALU.max, op1=ALU.add))
            v.tensor_scalar(aS[:].rearrange("p g b -> p (g b)"), sp[:, 7], con[:, C_ROW:C_ROW + 1],
                            con[:, C_ROW + 1:C_ROW + 2], ALU.mult, ALU.add).then_inc(aS_ready, 1)
            dve.wait_ge(r0_act, 4)
            link(v.tensor_tensor(s8[:, 5], s8[:, 4], s8[:, 3], ALU.mult))
            link(v.tensor_tensor(z8[:, 4].rearrange(h3, h=NH), hb0.rearrange(h3, h=NH),
                                 s8[:, 5].unsqueeze(2).broadcast_to([NB, NH, HD]), ALU.mult))
            total = TOPK * float(np.exp(-np.sqrt(1e-8)))
            link(v.scalar_tensor_tensor(out=z8[:, 5], in0=v0, scalar=total / (total + 1e-8), in1=z8[:, 4],
                                        op0=ALU.mult, op1=ALU.add))
            v.tensor_tensor(z8[:, 6], z8[:, 5], q0, ALU.mult).then_inc(r0_dve, 1)
            dve.wait_ge(r0_pe, 1)
            v.tensor_copy(o0T[:], psX[:, 128:128 + NB]).then_inc(r0_dve, 1)
            gate_weights(2)
            dve.wait_ge(r0_pe, 2)
            link(v.tensor_tensor(z8[:, 7], psX[0:NB, 256:384], gn[:, 0], ALU.mult))
            link(v.tensor_tensor(z8[:, 7], z8[:, 7], x0_sb[:], ALU.add))
            link(v.bn_stats(s8[:, 9, 0:6], z8[:, 7]))
            v.bn_aggr(s8[:, 6, 0:2], s8[:, 9, 0:6]).then_inc(r0_dve, 1)
            gate_weights(3)
            dve.wait_ge(r0_act, 6)
            v.tensor_scalar(z8[:, 8], z8[:, 7], s8[:, 6, 0:1], s8[:, 7, 1:2], ALU.subtract, ALU.mult).then_inc(r0_dve, 1)
            dve.wait_ge(r0_pe, 3)
            link(v.tensor_tensor(h0T[:], psX[:, 136:136 + NB], modT[:, 4], ALU.mult))
            v.tensor_tensor(h0T[:], h0T[:], modT[:, 3], ALU.add).then_inc(r0_dve, 1)

            def routing(i):
                if i == -1:
                    dve.wait_ge(r0_pe, 4)
                    lg = s8[:, 8]
                    link(v.tensor_copy(lg, psX[0:NB, 144:144 + NE]))
                    link(v.max(s8[:, 9], lg))
                    v.tensor_scalar(s8[:, 10, 0:1], s8[:, 9, 0:1], -1.0, None, ALU.mult).then_inc(r0_dve, 1)
                    link(v.tensor_scalar(s8[:, 12], lg, s8[:, 9, 1:2], None, ALU.is_gt))
                    link(v.tensor_scalar(s8[:, 13], lg, s8[:, 9, 1:2], None, ALU.is_equal))
                    link(v.tensor_copy(s8[:, 14], s8[:, 13]))
                    for sh in (1, 2, 4):
                        link(v.tensor_copy(s8[:, 15], s8[:, 14]))
                        link(v.tensor_tensor(s8[:, 14, sh:NE], s8[:, 14, sh:NE], s8[:, 15, 0:NE - sh], ALU.add))
                    link(v.tensor_reduce(s8[:, 16, 0:1], s8[:, 12], AX_X, ALU.add))
                    link(v.tensor_scalar(s8[:, 16, 1:2], s8[:, 16, 0:1], -1.0, 2.0, ALU.mult, ALU.add))
                    link(v.tensor_scalar(s8[:, 17], s8[:, 14], s8[:, 16, 1:2], None, ALU.is_le))
                    link(v.tensor_tensor(s8[:, 17], s8[:, 17], s8[:, 13], ALU.mult))
                    link(v.tensor_tensor(s8[:, 17], s8[:, 17], s8[:, 12], ALU.add))
                    dve.wait_ge(r0_act, 7)
                    link(v.tensor_tensor(s8[:, 18], s8[:, 11], s8[:, 17], ALU.mult))
                    link(v.tensor_reduce(s8[:, 19, 0:1], s8[:, 18], AX_X, ALU.add))
                    link(v.reciprocal(s8[:, 19, 1:2], s8[:, 19, 0:1]))
                    v.tensor_scalar(s8[:, 20], s8[:, 18], s8[:, 19, 1:2], None, ALU.mult).then_inc(r0_dve, 1)
                    dve.wait_ge(r0_pe, 5)
                    v.tensor_copy(gateT[:], psX[0:NE, 152:152 + NB]).then_inc(r0_dve, 1)
                    dve.wait_ge(r0_pe, 6)
                    v.tensor_copy(gate_er[:].rearrange("p k b -> p (k b)"), psX[:, 160:160 + 4 * NB]).then_inc(r0_dve, 1)
                if i == 0:
                    dve.wait_ge(r0_dve, 10)
                    for kt in range(2):
                        v.tensor_tensor(bsc[:, kt], b_sb[:, kt].unsqueeze(1).broadcast_to([P, NB, D]),
                                        gate_er[:, kt].unsqueeze(2).broadcast_to([P, NB, D]), ALU.mult).then_inc(bsc_ready, 1)
                if i == 1:
                    expert_matrices(0)

            def expert_matrices(half):
                four = slice(4 * half, 4 * half + 4)
                dve.wait_ge(pG_ready, half + 1)
                need(dve, gb_ready, half)
                link(v.tensor_tensor(mI[:], (psC, psX)[half][:].rearrange("p (b d) -> p b d", b=4),
                                     ident.unsqueeze(1).broadcast_to([P, 4, D]), ALU.add))
                v.tensor_tensor(g_b[:, four], g_b[:, four], mI[:], ALU.mult).then_inc(gb_ready, 1)

            def rounds(i, ph, rnd, between=None, late=None):
                s = ph % 2
                src = key[:, s] if rnd == 0 else work[:, s]
                for half in range(2):
                    wait_alone(dve, picked, 16 * i + 4 * (rnd - 1) + 3 + half)
                    for h in range(4 * half, 4 * half + 4):
                        last = v.max(m8[:, h], src[:, h * WIN:(h + 1) * WIN])
                    last.then_inc(picked, 1)
                if between:
                    between()
                for half in range(2):
                    wait_alone(dve, picked, 16 * i + 4 * rnd + 1 + half)
                    if late and half == 1:
                        late()
                    for h in range(4 * half, 4 * half + 4):
                        cols = slice(h * WIN, (h + 1) * WIN)
                        last = v.match_replace(work[:, s, cols], m8[:, h], src[:, cols], GONE)
                    last.then_inc(picked, 1)

            def step(i, ph):
                if there(i, 0):
                    dve.wait_ge(key_ready, i + 1)
                    rounds(i, ph, 0, lambda: wait_alone(dve, w_ready, 2 * (i - 1)))
                    if isinstance(i, int) and i == 1:
                        expert_matrices(1)
                if there(i, 0):
                    rounds(i, ph, 1)
                k, s = i + 1, (ph + 1) % 2
                if there(i, 1):
                    dve.wait_ge(qhs_ready, k + 1)
                    e = key[:, s].rearrange("p (h j) -> p h j", h=NH)
                    v.scalar_tensor_tensor(out=e, in0=pH[:, :, WIN:2 * WIN], scalar=0.0, in1=e, op0=ALU.max, op1=ALU.min).then_inc(d2_ready, 1)
                if there(i, 0):
                    rounds(i, ph, 2)
                if there(i, -2):
                    dve.wait_ge(x2_ready, i - 1)
                    v.bn_stats(st_c[:], x2[:, ph % 2]).then_inc(stc_ready, 1)

                def between():
                    if there(i, -2):
                        wait_alone(dve, stc_ready, i - 1)
                        wait_alone(dve, nc_ready, i - 3)
                        v.bn_aggr(mv_c[:, ph % 2], st_c[:]).then_inc(mvc_ready, 1)
                    if there(i, -1):
                        s = (ph - 1) % 2
                        dve.wait_ge(cst_ready, 2 * i)
                        need(dve, rden_ready, i - 2)
                        v.tensor_scalar(den[:, s], cst[:, s, :, HD], 1e-8, None, ALU.add).then_inc(den_done, 1)

                def late():
                    if there(i, -1):
                        dve.wait_ge(den_done, i)
                        v.reciprocal(rden[:, (ph - 1) % 2], den[:, (ph - 1) % 2]).then_inc(rden_ready, 1)

                if there(i, 0):
                    rounds(i, ph, 3, between, late)
                else:
                    between()
                    late()

            steps(dve, step, routing)

        @block.tensor
        def _(pe):
            mm = nc.tensor.matmul
            pe.wait_ge(sil_ready, 1)
            for j in range(6):
                last = mm(psC[:, j * NB:(j + 1) * NB], wmod_sb[:, j * D:(j + 1) * D], sil[:], start=True, stop=True)
            last.then_inc(pmod_ready, 1)
            for j in range(2):
                last = mm(psW[0:NB, j, 0:384], sil[:], wmod_sb[:, j * 384:(j + 1) * 384], start=True, stop=True)
            last.then_inc(pmod_ready, 1)
            pe.wait_ge(con_in, 16)
            pe.wait_ge(wq_in, 16)
            pe.wait_ge(modn_ready, 2)
            def to_pT(n, u):
                pe.wait_ge(xn_ready, n + 1)
                need(pe, hT_ready, n - 1)
                for c in range(4):
                    last = nc.tensor.transpose(psW[:, u % 2, c * P:(c + 1) * P], xn[:, u % 2, c], ident)
                last.then_inc(pT_ready, 1)

            def to_pq(n, u):
                pe.wait_ge(hT_ready, n + 1)
                for g in range(NG):
                    mm(psD[:, 2 * (u % 2) + g], encq_sb[:, g],
                       hT_all[:, bass.ds((n // 2) * TP + WIN + (n % 2) * HALF, HALF)],
                       start=True, stop=True).then_inc(pq_ready, 1)

            to_pT(0, 0)
            to_pT(1, 1)
            pe.wait_ge(diag_ready, 2 * NG)
            for g in range(NG):
                mm(psX[:, 384 + g * HD:384 + (g + 1) * HD], udiag[:, g].rearrange("k r e -> k (r e)"), hebv_sb[:],
                   start=True, stop=True)
                mm(psX[:, 256 + g * 64:320 + g * 64], udiag[:, g].rearrange("k r e -> k (r e)"),
                   vdiag[:, g].rearrange("k r e -> k (r e)"), start=True, stop=True).then_inc(pheb_ready, 1)
            to_pq(0, 0)
            with pe.Fori(1, 2 * NB - 6, 4) as n0:
                for u in range(4):
                    to_pT(n0 + u + 1, u)
                    to_pq(n0 + u, u + 1)
            for n in range(2 * NB - 3, 2 * NB):
                if n + 1 < 2 * NB:
                    to_pT(n + 1, n + 1)
                to_pq(n, n)

            def gate_rows(pr):
                pe.wait_ge(gates_n_ready, 1)
                need(pe, gatew_ready, pr)
                for j in range(2):
                    last = mm(psC[:, j * 256:(j + 1) * 256], con[0:NB, 2 * pr + j:2 * pr + j + 1].broadcast_to([NB, P]),
                              gn[:].rearrange("b u d -> b (u d)"), start=True, stop=True)
                last.then_inc(pgate_ready, 1)

            gate_rows(0)
            pe.wait_ge(wts_in, 16 * 13)
            pe.wait_ge(sig_ready, 1)
            pe.wait_ge(selheb_ready, 2 * NG + 2)
            for g in range(NG):
                last = mm(psX[0:64, 0:NB], w1_sb[:, g], sig[:, g], start=(g == 0), stop=(g == NG - 1))
            last.then_inc(pm1_ready, 1)
            pe.wait_ge(q_ready, 4 * NB)
            first = slice(WIN, NB * TP, TP)
            for g in range(NG):
                o = psW[0:NB, 1, 0:256].rearrange("p (a r g e) -> p a r g e", a=2, r=NR, g=NG)[:, :, :, g]
                mm(o, qT_all[:, g, first], selheb[:, g].rearrange("p a (r e) -> p a r e", r=NR), start=True, stop=True)
            mm(psW[0:NB, 1, 256:384], hT_all[:, first], encv_sb[:], start=True, stop=True).then_inc(p0_ready, 1)
            pe.wait_ge(h1_ready, 1)
            for g in range(NG):
                last = mm(psX[:, 64 + g * NB:64 + (g + 1) * NB], w2_sb[:, g], h1[:], start=True, stop=True)
            last.then_inc(pm2_ready, 1)
            gate_rows(1)
            gate_rows(2)
            pe.wait_ge(bf_set, 2)
            pe.wait_ge(ones_set, 8)
            pe.wait_ge(ones_in, 16 * NR)

            def routing(i):
                if i == -2:
                    pe.wait_ge(z_ready, 1)
                    pe.wait_ge(r0_dve, 2)
                    nc.tensor.transpose(psX[:, 128:128 + NB], z8[:, 6], con[0:NB, 0:NB]).then_inc(r0_pe, 1)
                    pe.wait_ge(r0_dve, 3)
                    mm(psX[0:NB, 256:384], o0T[:], dec_sb[:], start=True, stop=True).then_inc(r0_pe, 1)
                    gate_rows(3)
                    pe.wait_ge(r0_dve, 5)
                    nc.tensor.transpose(psX[:, 136:136 + NB], z8[:, 8], con[0:NB, 0:NB]).then_inc(r0_pe, 1)
                    pe.wait_ge(r0_dve, 6)
                    mm(psX[0:NB, 144:144 + NE], h0T[:], wr_sb[:], start=True, stop=True).then_inc(r0_pe, 1)
                if i == -1:
                    pe.wait_ge(r0_dve, 8)
                    nc.tensor.transpose(psX[0:NE, 152:152 + NB], s8[:, 20], con[0:NB, 0:NB]).then_inc(r0_pe, 1)
                    pe.wait_ge(r0_dve, 9)
                    for kt in range(4):
                        last = mm(psX[:, 160 + kt * NB:160 + (kt + 1) * NB], con[0:NE, C_EXP + kt * P:C_EXP + (kt + 1) * P],
                                  gateT[:], start=True, stop=True)
                    last.then_inc(r0_pe, 1)
                if i == 0:
                    pe.wait_ge(bsc_ready, 4)
                    pe.wait_ge(gatew_ready, NB // 2)
                    for half, bank in enumerate((psC, psX)):
                        for kt in range(4):
                            last = mm(bank[:], a_sb[:, kt], bsc[:, kt, 4 * half:4 * half + 4].rearrange("p b d -> p (b d)"),
                                      start=(kt == 0), stop=(kt == 3))
                        last.then_inc(pG_ready, 1)

            def bank_of(r):
                return psD[:, r].rearrange("p (g x) -> p g x", g=NG)

            def distances(s, r):
                mm(bank_of(r)[:, :, 0:SW], ident_bf[:], mask_bf[:].unsqueeze(1).broadcast_to([P, NG, SW]), start=True,
                   stop=False, skip_group_check=True)
                for g in range(NG):
                    last = mm(bank_of(r)[:, g, 0:SW], tst[:, s, r, g], sst[:, s, g], start=False, stop=(g == NG - 1),
                              skip_group_check=True)
                return last

            def step(i, ph):
                def weights_T(w):
                    k, s = i - 1, (ph - 1) % 2
                    if there(i, -1):
                        pe.wait_ge(w_ready, 2 * k + 1 + w)
                        if w == 0:
                            need(pe, nst_ready, min(k + 4, NCH) if isinstance(k, int) else k + 4)
                        need(pe, wts_ready, 2 * k - 1 + w)
                        if w == 1:
                            need(pe, vst_ready, min(k + 3, NCH) if isinstance(k, int) else k + 3)
                        for h in range(4 * w, 4 * w + 4):
                            nc.tensor.transpose(psW[:, w, (h % 4) * P:(h % 4 + 1) * P], wun[:, s, h],
                                                ident).then_inc(wt_ready, 1)

                weights_T(0)
                s, x4 = ph % 2, (ph - 2) % 4
                if there(i, -2):
                    k = i - 2
                    pe.wait_ge(xs_in[x4], 16 * (k // 4) + 16)
                    pe.wait_ge(oT_ready, k + 1)
                    mm(pAtt, ident, xs[:, x4], start=True, stop=False)
                    mm(pAtt, oT[:, s], dec_b[:, bass.ds(k // CPB, 1)].squeeze(1), start=False, stop=True).then_inc(att_ready, 1)
                weights_T(1)
                k, s = i - 3, (ph - 3) % 2
                if there(i, -3):
                    pe.wait_ge(nc_ready, k + 1)
                    need(pe, x2_ready, min(k + 2, NCH) if isinstance(k, int) else k + 2)
                    nc.tensor.transpose(pN2, n_c[:, s], ident).then_inc(pn2_ready, 1)
                k, s, s4 = i - 1, (ph - 1) % 2, (ph - 1) % 4
                if there(i, -1):
                    if isinstance(i, int) and i == 1:
                        pe.wait_ge(gb_ready, 2)
                    need(pe, cst_ready, 2 * k)
                    pe.wait_ge(vst_ready, k + 1)
                    for h in range(NH):
                        if h % 4 == 0:
                            pe.wait_ge(wts_ready, 2 * k + 1 + h // 4)
                        last = mm(pC[:, h * 2 * VD:(h + 1) * 2 * VD], wts[:, s, h],
                                  vst[:, s4, h].rearrange("p v e -> p (v e)"), start=True, stop=True)
                    last.then_inc(c_ready, 1)
                k, s = i - 3, (ph - 3) % 2
                if there(i, -3):
                    pe.wait_ge(h2T_ready, k + 1)
                    mm(pY, ident, x2[:, s], start=True, stop=False)
                    mm(pY, h2T[:, s], g_b[:, bass.ds(k // CPB, 1)].squeeze(1), start=False, stop=True).then_inc(y_ready, 1)
                k, s = i + 3, (ph + 3) % 2
                if there(i, 3):
                    pe.wait_ge(opnd_ready, 3 * (k + 1))
                    need(pe, nst_ready, k)
                    need(pe, wts_ready, 2 * (k - 3))
                    for g in range(NG):
                        mm(pN, selm[:, s, g], sqs[:, s, g], start=(g == 0), stop=(g == NG - 1))
                    for g in range(NG):
                        last = mm(pNN, sqs[:, s, g, WIN:3 * WIN], seln[:, g], start=(g == 0), stop=(g == NG - 1))
                    last.then_inc(pn_ready, 1)
                k, s = i + 2, (ph + 2) % 2
                if there(i, 2):
                    pe.wait_ge(rows_in[s], ROWS_IN * (k // 2) + ROWS_IN)
                    need(pe, vst_ready, k)
                    need(pe, wts_ready, 2 * (k - 2))
                    for v in range(2):
                        last = mm(pV[:, v], hst[:, s, v * WIN:(v + 2) * WIN], encv_sb[:], start=True, stop=True)
                    last.then_inc(v_ready, 1)
                    need(pe, d2_ready, k)
                    for r in range(NR - 1):
                        distances(s, r)
                if there(i, -1):
                    pe.wait_ge(osp_ready, i)
                    need(pe, yo_ready, i - 2)
                    nc.tensor.transpose(pO, osp[:, (ph - 1) % 2], ident).then_inc(po_ready, 1)
                if there(i, 2):
                    distances(s, NR - 1).then_inc(dist_ready, 1)

            steps(pe, step, routing)


def kernel(**inputs):
    import concourse.bacc as bacc
    from concourse.bass_utils import run_bass_kernel_spmd

    a = {k.replace("L0_", ""): np.asarray(v) for k, v in inputs.items()}

    def padded(w):
        w = w.reshape(w.shape[:-1] + (NR, NG, HD))
        w = np.moveaxis(w, -2, -3)
        w = np.pad(w, [(0, 0)] * (w.ndim - 1) + [(0, 32 - HD)])
        return w.reshape(w.shape[:-3] + (NG, P))

    encq = a["attn_enc_q"].transpose(1, 0, 2).reshape(D, P)
    arrays = {
        "x": a["attn_x"].reshape(NB * T, D),
        "encq": padded(encq),
        "encv": a["attn_enc_v"].transpose(0, 2, 1).reshape(P, D).T,
        "w1": padded(a["attn_metric_w1"].T).transpose(2, 1, 0),
        "b1": a["attn_metric_b1"].reshape(64, 1),
        "w2": padded(a["attn_metric_w2"]),
        "b2": padded(a["attn_metric_b2"]).T,
        "base": padded(a["attn_base_metric"].reshape(P)).T,
        "hebu": a["attn_hebb_U"].transpose(0, 2, 1).reshape(NH * RANK, HD),
        "hebv": a["attn_hebb_V"].reshape(NH * RANK, HD),
        "dec": a["attn_decoder"],
        "wr": a["ffn_Wr"].T,
        "amat": a["ffn_A"].reshape(4, P, D).transpose(1, 0, 2),
        "bmat": a["ffn_Bw"].transpose(0, 2, 1).reshape(4, P, D).transpose(1, 0, 2),
        "cin": a["c"].T,
        "wmod": a["wmod"],
        "consts": constants(),
    }
    nc = bacc.Bacc("TRN2", target_bir_lowering=False, num_devices=1)
    arrays = {f"in_{k}": np.ascontiguousarray(v) for k, v in arrays.items()}
    args = [nc.dram_tensor(k, v.shape, F32, kind="ExternalInput").ap() for k, v in arrays.items()]
    args.append(nc.dram_tensor("out_0", (NB * T, D), F32, kind="ExternalOutput").ap())
    adaln_block(nc, *args)
    r = run_bass_kernel_spmd(nc, [arrays], core_ids=[0])
    return r.results[0]["out_0"].reshape(NB, T, D)
```
